# Optimizing a Trainium2 kernel written in Bass

```python
import numpy as np
import jax
import jax.numpy as jnp

def _softmax(x, axis=-1):
    return jax.nn.softmax(x, axis=axis)

def _gelu(x):
    return jax.nn.gelu(x, approximate=True)

def _silu(x):
    return jax.nn.silu(x)

def _sigmoid(x):
    return jax.nn.sigmoid(x)

def _layernorm(x, axis=-1, eps=1e-05):
    m = jnp.mean(x, axis=axis, keepdims=True)
    v = jnp.var(x, axis=axis, keepdims=True)
    return (x - m) / jnp.sqrt(v + eps)

def _scatter_add(tgt, idx, src, axis=0):
    return tgt.at[idx].add(src)

def _segment_sum(src, seg, n):
    return jax.ops.segment_sum(src, seg, n)
kernel_name = 'mk_perceiver_d2_seqx_r2_5f44da'

def setup_inputs(seed: int=0):
    np.random.seed(seed)
    _w = jnp.asarray

    def _rec_inputs():
        import jax
        import jax.numpy as jnp
        _rk = jax.random.key(seed)
        x = -0.0003929 + 0.9999 * jax.random.normal(jax.random.fold_in(_rk, 1), (1, 256, 512), jnp.float32)
        _lenS = 256 - jax.random.randint(jax.random.fold_in(_rk, 7), (1,), 0, max(1, 256 // 4) + 1, jnp.int32)
        _lenS2 = 25088 - jax.random.randint(jax.random.fold_in(_rk, 8), (1,), 0, max(1, 25088 // 4) + 1, jnp.int32)
        _ctx_1024P = jax.random.normal(jax.random.fold_in(_rk, 11), (1, 16, 512), jnp.float32)
        _ctx_1024c = jax.random.dirichlet(jax.random.fold_in(_rk, 511), 0.3 * jnp.ones((16,), jnp.float32), (1, 25088))
        _ctx_1024t = jnp.einsum('bsk,bkd->bsd', _ctx_1024c, _ctx_1024P)
        _ctx_1024t = _ctx_1024t * jax.lax.rsqrt(jnp.mean(jnp.square(_ctx_1024t)) + 1e-12) * 0.953939
        ctx_1024 = 2.81802e-05 + 1.00001 * (_ctx_1024t + 0.3 * jax.random.normal(jax.random.fold_in(_rk, 611), (1, 25088, 512), jnp.float32))
        return (x, ctx_1024)
    x, ctx_1024 = _rec_inputs()

    def _L0_xattn_setup():
        import jax, jax.numpy as jnp
        import numpy as np
        D1, D2, D3 = (512, 512, 512)
        key = jax.random.key(seed)
        k1, k2, kw, kb = jax.random.split(key, 4)
        x1 = jax.random.normal(k1, (8, 1024, D1), dtype=jnp.float32)
        x2 = jax.random.normal(k2, (8, 1024, D2), dtype=jnp.float32)
        bound = 1.0 / np.sqrt(D1 + D2)
        W = jax.random.uniform(kw, (D3, D1 + D2), minval=-bound, maxval=bound, dtype=jnp.float32)
        b = jax.random.uniform(kb, (D3,), minval=-bound, maxval=bound, dtype=jnp.float32)
        return {'x1': x1, 'x2': x2, 'W': W, 'b': b}
    _L0_xattn_all = _L0_xattn_setup()
    _L0_xattn_in = {k: v for k, v in _L0_xattn_all.items() if k in ('W', 'b')}
    del _L0_xattn_all

    def _L0_attn_setup():
        import jax, jax.numpy as jnp
        import numpy as np
        B, T, D = (2, 1024, 512)
        H, W = (16, 128)
        HD = D // H
        key = jax.random.key(seed)
        ks = jax.random.split(key, 5)
        s = 0.02
        return {'x': jax.random.normal(ks[0], (B, T, D), dtype=jnp.float32), 'Wqkv': jax.random.normal(ks[1], (3 * D, D), dtype=jnp.float32) * s, 'bqkv': jax.random.normal(ks[2], (3 * D,), dtype=jnp.float32) * s, 'Wo': jax.random.normal(ks[3], (D, D), dtype=jnp.float32) * s, 'bo': jax.random.normal(ks[4], (D,), dtype=jnp.float32) * s}
    _L0_attn_all = _L0_attn_setup()
    _L0_attn_in = {k: v for k, v in _L0_attn_all.items() if k in ('Wqkv', 'bqkv', 'Wo', 'bo')}
    del _L0_attn_all

    def _L0_ffn_setup():
        import jax, jax.numpy as jnp
        import numpy as np
        B, S, H = (1, 1024, 512)
        E = 16
        I = 384
        TOPK = 4
        G = 4
        TOPK_G = 2
        SCALE = 2.5
        N_SHARED = 1

        def _route(x, gate_w, gate_bias):
            n = x.shape[0]
            logits = jnp.einsum('nh,eh->ne', x.astype(jnp.float32), gate_w)
            scores = jax.nn.sigmoid(logits)
            sb = scores + gate_bias
            gs = sb.reshape(n, G, E // G)
            group_scores = jnp.sum(jax.lax.top_k(gs, 2)[0], axis=-1)
            _, gidx = jax.lax.top_k(group_scores, TOPK_G)
            gmask = jnp.sum(jax.nn.one_hot(gidx, G, dtype=sb.dtype), axis=1)
            emask = jnp.repeat(gmask, E // G, axis=-1)
            masked = jnp.where(emask > 0, sb, -jnp.inf)
            _, tidx = jax.lax.top_k(masked, TOPK)
            w = jnp.take_along_axis(scores, tidx, axis=1)
            w = w / (jnp.sum(w, axis=-1, keepdims=True) + 1e-20)
            return (tidx, w * SCALE)
        key = jax.random.key(seed)
        ks = jax.random.split(key, 9)

        def rn(k, shape, scale=0.02):
            return jax.random.normal(k, shape, dtype=jnp.float32) * scale
        return dict(hidden_states=jax.random.normal(ks[0], (B, S, H), dtype=jnp.float32), gate_w=rn(ks[1], (E, H)), gate_bias=jax.random.normal(ks[2], (E,), dtype=jnp.float32) * 0.1, w1=rn(ks[3], (E, I, H)), w2=rn(ks[4], (E, H, I)), w3=rn(ks[5], (E, I, H)), ws1=rn(ks[6], (I * N_SHARED, H)), ws2=rn(ks[7], (H, I * N_SHARED)), ws3=rn(ks[8], (I * N_SHARED, H)))
    _L0_ffn_all = _L0_ffn_setup()
    _L0_ffn_in = {k: v for k, v in _L0_ffn_all.items() if k in ('gate_w', 'gate_bias', 'w1', 'w2', 'w3', 'ws1', 'ws2', 'ws3')}
    del _L0_ffn_all

    def _L1_xattn_setup():
        import jax, jax.numpy as jnp
        import numpy as np
        D_MODEL = 512
        HEADS = 16
        D_K = D_MODEL // HEADS
        SCALE = 1.0 / np.sqrt(D_K)

        def _proj(x, W, b):
            B, S, _ = x.shape
            return (x @ W + b).reshape(B, S, HEADS, D_K)
        key = jax.random.key(seed)
        ks = jax.random.split(key, 12)
        B, S = (4, 1024)
        std = 1.0 / np.sqrt(D_MODEL)
        inp = {'query': jax.random.normal(ks[0], (B, S, D_MODEL), jnp.float32), 'key': jax.random.normal(ks[1], (B, S, D_MODEL), jnp.float32), 'value': jax.random.normal(ks[2], (B, S, D_MODEL), jnp.float32), 'Wq': jax.random.normal(ks[3], (D_MODEL, D_MODEL), jnp.float32) * std, 'bq': jax.random.normal(ks[4], (D_MODEL,), jnp.float32) * std, 'Wk': jax.random.normal(ks[5], (D_MODEL, D_MODEL), jnp.float32) * std, 'bk': jax.random.normal(ks[6], (D_MODEL,), jnp.float32) * std, 'Wv': jax.random.normal(ks[7], (D_MODEL, D_MODEL), jnp.float32) * std, 'bv': jax.random.normal(ks[8], (D_MODEL,), jnp.float32) * std, 'Wo': jax.random.normal(ks[9], (D_MODEL, D_MODEL), jnp.float32) * std, 'bo': jax.random.normal(ks[10], (D_MODEL,), jnp.float32) * std}
        return inp
    _L1_xattn_all = _L1_xattn_setup()
    _L1_xattn_in = {k: v for k, v in _L1_xattn_all.items() if k in ('Wq', 'bq', 'Wk', 'bk', 'Wv', 'bv', 'Wo', 'bo')}
    del _L1_xattn_all

    def _L1_attn_setup():
        import jax, jax.numpy as jnp
        import numpy as np
        D_MODEL = 512
        NUM_HEADS = 16
        WINDOW = 128
        DISP = WINDOW // 2
        SHIFTED = True
        NEG = -9000000000000000.0

        def _create_mask(w):
            m = np.ones((w, w), dtype=np.float32)
            m[:DISP, -DISP:] = 0.0
            m[-DISP:, :DISP] = 0.0
            return jnp.asarray(m)
        key = jax.random.key(seed)
        ks = jax.random.split(key, 5)
        b, s, d = (4, 4096, D_MODEL)
        sc = 1.0 / np.sqrt(d)
        return {'x': jax.random.normal(ks[0], (b, s, d), jnp.float32), 'w_qkv': jax.random.normal(ks[1], (d, 3 * d), jnp.float32) * sc, 'b_qkv': jax.random.normal(ks[2], (3 * d,), jnp.float32) * 0.02, 'w_o': jax.random.normal(ks[3], (d, d), jnp.float32) * sc, 'b_o': jax.random.normal(ks[4], (d,), jnp.float32) * 0.02}
    _L1_attn_all = _L1_attn_setup()
    _L1_attn_in = {k: v for k, v in _L1_attn_all.items() if k in ('w_qkv', 'b_qkv', 'w_o', 'b_o')}
    del _L1_attn_all

    def _L1_ffn_setup():
        import jax, jax.numpy as jnp
        import numpy as np
        TOP_K = 2
        TEMP = 0.9
        EPS = 1e-05
        B, S, D, F, E = (2, 1024, 512, 2048, 8)

        def _moe_forward(x, gate_w, gate_b, w1, b1, w2, b2, ln_g, ln_b):
            logits = (x @ gate_w + gate_b) / TEMP
            topk_vals, topk_idx = jax.lax.top_k(logits, TOP_K)
            keep = jax.nn.one_hot(topk_idx, E, dtype=jnp.bool_).any(-2)
            masked = jnp.where(keep, logits, -jnp.inf)
            gate_probs = jax.nn.softmax(masked, axis=-1)
            h = jnp.einsum('bsd,edf->bsef', x, w1) + b1
            h = jax.nn.gelu(h, approximate=False)
            expert_out = jnp.einsum('bsef,efd->bsed', h, w2) + b2
            out = jnp.einsum('bse,bsed->bsd', gate_probs, expert_out)
            mu = out.mean(-1, keepdims=True)
            var = out.var(-1, keepdims=True)
            out = (out - mu) / jnp.sqrt(var + EPS) * ln_g + ln_b
            return out
        key = jax.random.key(seed)
        ks = jax.random.split(key, 4)
        scale_in = 1.0 / np.sqrt(D)
        scale_ff = 1.0 / np.sqrt(F)
        return {'x': jax.random.normal(ks[0], (B, S, D), jnp.float32), 'gate_w': jax.random.normal(ks[1], (D, E), jnp.float32) * scale_in, 'gate_b': jnp.zeros((E,), jnp.float32), 'w1': jax.random.normal(ks[2], (E, D, F), jnp.float32) * scale_in, 'b1': jnp.zeros((E, F), jnp.float32), 'w2': jax.random.normal(ks[3], (E, F, D), jnp.float32) * scale_ff, 'b2': jnp.zeros((E, D), jnp.float32), 'ln_g': jnp.ones((D,), jnp.float32), 'ln_b': jnp.zeros((D,), jnp.float32)}
    _L1_ffn_all = _L1_ffn_setup()
    _L1_ffn_in = {k: v for k, v in _L1_ffn_all.items() if k in ('gate_w', 'gate_b', 'w1', 'b1', 'w2', 'b2', 'ln_g', 'ln_b')}
    del _L1_ffn_all
    return {'x': x, 'ctx_1024': ctx_1024, 'L0_xattn_W': _L0_xattn_in['W'], 'L0_xattn_b': _L0_xattn_in['b'], 'L0_attn_Wqkv': _L0_attn_in['Wqkv'], 'L0_attn_bqkv': _L0_attn_in['bqkv'], 'L0_attn_Wo': _L0_attn_in['Wo'], 'L0_attn_bo': _L0_attn_in['bo'], 'L0_ffn_gate_w': _L0_ffn_in['gate_w'], 'L0_ffn_gate_bias': _L0_ffn_in['gate_bias'], 'L0_ffn_w1': _L0_ffn_in['w1'], 'L0_ffn_w2': _L0_ffn_in['w2'], 'L0_ffn_w3': _L0_ffn_in['w3'], 'L0_ffn_ws1': _L0_ffn_in['ws1'], 'L0_ffn_ws2': _L0_ffn_in['ws2'], 'L0_ffn_ws3': _L0_ffn_in['ws3'], 'L1_xattn_Wq': _L1_xattn_in['Wq'], 'L1_xattn_bq': _L1_xattn_in['bq'], 'L1_xattn_Wk': _L1_xattn_in['Wk'], 'L1_xattn_bk': _L1_xattn_in['bk'], 'L1_xattn_Wv': _L1_xattn_in['Wv'], 'L1_xattn_bv': _L1_xattn_in['bv'], 'L1_xattn_Wo': _L1_xattn_in['Wo'], 'L1_xattn_bo': _L1_xattn_in['bo'], 'L1_attn_w_qkv': _L1_attn_in['w_qkv'], 'L1_attn_b_qkv': _L1_attn_in['b_qkv'], 'L1_attn_w_o': _L1_attn_in['w_o'], 'L1_attn_b_o': _L1_attn_in['b_o'], 'L1_ffn_gate_w': _L1_ffn_in['gate_w'], 'L1_ffn_gate_b': _L1_ffn_in['gate_b'], 'L1_ffn_w1': _L1_ffn_in['w1'], 'L1_ffn_b1': _L1_ffn_in['b1'], 'L1_ffn_w2': _L1_ffn_in['w2'], 'L1_ffn_b2': _L1_ffn_in['b2'], 'L1_ffn_ln_g': _L1_ffn_in['ln_g'], 'L1_ffn_ln_b': _L1_ffn_in['ln_b']}

def reference(x, ctx_1024, L0_xattn_W, L0_xattn_b, L0_attn_Wqkv, L0_attn_bqkv, L0_attn_Wo, L0_attn_bo, L0_ffn_gate_w, L0_ffn_gate_bias, L0_ffn_w1, L0_ffn_w2, L0_ffn_w3, L0_ffn_ws1, L0_ffn_ws2, L0_ffn_ws3, L1_xattn_Wq, L1_xattn_bq, L1_xattn_Wk, L1_xattn_bk, L1_xattn_Wv, L1_xattn_bv, L1_xattn_Wo, L1_xattn_bo, L1_attn_w_qkv, L1_attn_b_qkv, L1_attn_w_o, L1_attn_b_o, L1_ffn_gate_w, L1_ffn_gate_b, L1_ffn_w1, L1_ffn_b1, L1_ffn_w2, L1_ffn_b2, L1_ffn_ln_g, L1_ffn_ln_b):
    import jax
    import jax.numpy as jnp

    def _L0_xattn_ref(x1, x2, W, b):
        import jax, jax.numpy as jnp
        import numpy as np
        D1, D2, D3 = (512, 512, 512)
        d1 = x1.shape[-1]
        W1 = W[:, :d1]
        W2 = W[:, d1:]
        part1 = jnp.einsum('bld,ed->ble', x1, W1)
        part2 = jnp.einsum('bld,ed->be', x2, W2) / x2.shape[1]
        return part1 + part2[:, None, :] + b

    def _L0_attn_ref(x, Wqkv, bqkv, Wo, bo):
        import jax, jax.numpy as jnp
        import numpy as np
        B, T, D = (2, 1024, 512)
        H, W = (16, 128)
        HD = D // H
        b, t, d = x.shape
        qkv = x @ Wqkv.T + bqkv
        qkv = qkv.reshape(b, t, 3, H, HD)
        q = jnp.transpose(qkv[:, :, 0], (0, 2, 1, 3))
        k = jnp.transpose(qkv[:, :, 1], (0, 2, 1, 3))
        v = jnp.transpose(qkv[:, :, 2], (0, 2, 1, 3))
        scores = jnp.einsum('bhid,bhjd->bhij', q, k) / jnp.sqrt(jnp.float32(HD))
        i = jnp.arange(t)[:, None]
        j = jnp.arange(t)[None, :]
        mask = (j <= i) & (j >= i - (W - 1))
        scores = jnp.where(mask, scores, -jnp.inf)
        probs = jax.nn.softmax(scores, axis=-1)
        y = jnp.einsum('bhij,bhjd->bhid', probs, v)
        y = jnp.transpose(y, (0, 2, 1, 3)).reshape(b, t, d)
        return y @ Wo.T + bo

    def _L0_ffn_ref(hidden_states, gate_w, gate_bias, w1, w2, w3, ws1, ws2, ws3):
        import jax, jax.numpy as jnp
        import numpy as np
        B, S, H = (1, 1024, 512)
        E = 16
        I = 384
        TOPK = 4
        G = 4
        TOPK_G = 2
        SCALE = 2.5
        N_SHARED = 1

        def _route(x, gate_w, gate_bias):
            n = x.shape[0]
            logits = jnp.einsum('nh,eh->ne', x.astype(jnp.float32), gate_w)
            scores = jax.nn.sigmoid(logits)
            sb = scores + gate_bias
            gs = sb.reshape(n, G, E // G)
            group_scores = jnp.sum(jax.lax.top_k(gs, 2)[0], axis=-1)
            _, gidx = jax.lax.top_k(group_scores, TOPK_G)
            gmask = jnp.sum(jax.nn.one_hot(gidx, G, dtype=sb.dtype), axis=1)
            emask = jnp.repeat(gmask, E // G, axis=-1)
            masked = jnp.where(emask > 0, sb, -jnp.inf)
            _, tidx = jax.lax.top_k(masked, TOPK)
            w = jnp.take_along_axis(scores, tidx, axis=1)
            w = w / (jnp.sum(w, axis=-1, keepdims=True) + 1e-20)
            return (tidx, w * SCALE)
        b, s, h = hidden_states.shape
        x = hidden_states.reshape(-1, h)
        tidx, tw = _route(x, gate_w, gate_bias)
        n = x.shape[0]
        combine = jnp.zeros((n, E), x.dtype).at[jnp.arange(n)[:, None], tidx].add(tw)
        g = jnp.einsum('nh,eih->nei', x, w1)
        u = jnp.einsum('nh,eih->nei', x, w3)
        hact = jax.nn.silu(g) * u * combine[:, :, None]
        y = jnp.einsum('nei,ehi->nh', hact, w2)
        shared = jnp.einsum('ni,hi->nh', jax.nn.silu(x @ ws1.T) * (x @ ws3.T), ws2)
        return (y + shared).reshape(b, s, h)

    def _L1_xattn_ref(query, key, value, Wq, bq, Wk, bk, Wv, bv, Wo, bo):
        import jax, jax.numpy as jnp
        import numpy as np
        D_MODEL = 512
        HEADS = 16
        D_K = D_MODEL // HEADS
        SCALE = 1.0 / np.sqrt(D_K)

        def _proj(x, W, b):
            B, S, _ = x.shape
            return (x @ W + b).reshape(B, S, HEADS, D_K)
        B, S, _ = query.shape
        Q = _proj(query, Wq, bq)
        K = _proj(key, Wk, bk)
        V = _proj(value, Wv, bv)
        scores = jnp.einsum('bihd,bjhd->bijh', Q, K) * SCALE
        attn = jax.nn.softmax(scores, axis=1)
        x = jnp.einsum('bijh,bjhd->bihd', attn, V).reshape(B, S, D_MODEL)
        return x @ Wo + bo

    def _L1_attn_ref(x, w_qkv, b_qkv, w_o, b_o):
        import jax, jax.numpy as jnp
        import numpy as np
        D_MODEL = 512
        NUM_HEADS = 16
        WINDOW = 128
        DISP = WINDOW // 2
        SHIFTED = True
        NEG = -9000000000000000.0

        def _create_mask(w):
            m = np.ones((w, w), dtype=np.float32)
            m[:DISP, -DISP:] = 0.0
            m[-DISP:, :DISP] = 0.0
            return jnp.asarray(m)
        b, s, d = x.shape
        h, w = (NUM_HEADS, WINDOW)
        d_k = d // h
        if SHIFTED:
            x = jnp.roll(x, -DISP, axis=1)
        xw = x.reshape(-1, w, d)
        n = xw.shape[0]
        qkv = xw @ w_qkv + b_qkv
        qkv = qkv.reshape(n, w, h, d_k, 3)
        qkv = qkv.transpose(0, 2, 1, 3, 4).reshape(n, h, w, 3 * d_k)
        q, k, v = jnp.split(qkv, 3, axis=-1)
        attn = jnp.einsum('nhqd,nhkd->nhqk', q, k) / jnp.sqrt(jnp.float32(d_k))
        if SHIFTED:
            mask = _create_mask(w)
            attn = jnp.where(mask == 0, jnp.float32(NEG), attn)
        attn = jax.nn.softmax(attn, axis=-1)
        vals = jnp.einsum('nhqk,nhkd->nhqd', attn, v)
        vals = vals.transpose(0, 2, 1, 3).reshape(n, w, d)
        out = vals @ w_o + b_o
        out = out.reshape(b, s, d)
        if SHIFTED:
            out = jnp.roll(out, DISP, axis=1)
        return out

    def _L1_ffn_ref(x, gate_w, gate_b, w1, b1, w2, b2, ln_g, ln_b):
        import jax, jax.numpy as jnp
        import numpy as np
        TOP_K = 2
        TEMP = 0.9
        EPS = 1e-05
        B, S, D, F, E = (2, 1024, 512, 2048, 8)

        def _moe_forward(x, gate_w, gate_b, w1, b1, w2, b2, ln_g, ln_b):
            logits = (x @ gate_w + gate_b) / TEMP
            topk_vals, topk_idx = jax.lax.top_k(logits, TOP_K)
            keep = jax.nn.one_hot(topk_idx, E, dtype=jnp.bool_).any(-2)
            masked = jnp.where(keep, logits, -jnp.inf)
            gate_probs = jax.nn.softmax(masked, axis=-1)
            h = jnp.einsum('bsd,edf->bsef', x, w1) + b1
            h = jax.nn.gelu(h, approximate=False)
            expert_out = jnp.einsum('bsef,efd->bsed', h, w2) + b2
            out = jnp.einsum('bse,bsed->bsd', gate_probs, expert_out)
            mu = out.mean(-1, keepdims=True)
            var = out.var(-1, keepdims=True)
            out = (out - mu) / jnp.sqrt(var + EPS) * ln_g + ln_b
            return out
        return _moe_forward(x, gate_w, gate_b, w1, b1, w2, b2, ln_g, ln_b)
    x = x + _L0_xattn_ref(_layernorm(x, axis=-1), ctx_1024, L0_xattn_W, L0_xattn_b)
    x = x + _L0_attn_ref(_layernorm(x, axis=-1), L0_attn_Wqkv, L0_attn_bqkv, L0_attn_Wo, L0_attn_bo)
    x = x + _L0_ffn_ref(_layernorm(x, axis=-1), L0_ffn_gate_w, L0_ffn_gate_bias, L0_ffn_w1, L0_ffn_w2, L0_ffn_w3, L0_ffn_ws1, L0_ffn_ws2, L0_ffn_ws3)
    x = x + _L1_xattn_ref(_layernorm(x, axis=-1), ctx_1024, ctx_1024, L1_xattn_Wq, L1_xattn_bq, L1_xattn_Wk, L1_xattn_bk, L1_xattn_Wv, L1_xattn_bv, L1_xattn_Wo, L1_xattn_bo)
    x = x + _L1_attn_ref(_layernorm(x, axis=-1), L1_attn_w_qkv, L1_attn_b_qkv, L1_attn_w_o, L1_attn_b_o)
    x = x + _L1_ffn_ref(_layernorm(x, axis=-1), L1_ffn_gate_w, L1_ffn_gate_b, L1_ffn_w1, L1_ffn_b1, L1_ffn_w2, L1_ffn_b2, L1_ffn_ln_g, L1_ffn_ln_b)
    return x

_drawn_inputs = setup_inputs


def setup_inputs(seed=0):
    import zlib

    import numpy as np

    out = dict(_drawn_inputs(seed))
    spreads = {'L1_ffn_gate_b': (0.0, 2.0),
     'L1_ffn_b1': (0.0, 2.0),
     'L1_ffn_b2': (0.0, 2.0),
     'L1_ffn_ln_g': (1.0, 0.6),
     'L1_ffn_ln_b': (0.0, 2.0)}
    factors = {'L0_xattn_b': 27.492,
     'L0_attn_bqkv': 48.606,
     'L0_attn_bo': 23.554,
     'L1_xattn_bq': 200.0,
     'L1_xattn_bo': 64.0,
     'L1_attn_w_qkv': 3.796,
     'L1_attn_b_qkv': 28.742,
     'L1_attn_w_o': 4.298,
     'L1_attn_b_o': 173.081,
     'L1_ffn_gate_w': 40.813,
     'L1_ffn_w1': 32.855,
     'L1_ffn_w2': 3.436,
     'L0_ffn_gate_w': 2.776,
     'L0_ffn_gate_bias': 3.604,
     'L0_ffn_ws1': 2.93,
     'L0_ffn_ws2': 2.905,
     'L0_ffn_ws3': 2.832}
    for name, (base, spread) in spreads.items():
        noise = np.random.default_rng([zlib.crc32(name.encode()), seed]).standard_normal(out[name].shape)
        drawn = base * np.exp(spread * noise) if base else spread * noise
        out[name] = jnp.asarray(drawn.astype(out[name].dtype))
    for name, factor in factors.items():
        out[name] = (out[name] * factor).astype(out[name].dtype)
    return out
```

```python
from contextlib import ExitStack

import numpy as np

import concourse.bass as bass
from concourse import mybir

P = 128
F32 = mybir.dt.float32
F32R = mybir.dt.float32r
ALU = mybir.AluOpType
ACT = mybir.ActivationFunctionType
AX = mybir.AxisListType

D = 512
NC = 4
NCTX = 25088
GT = 256
NG = NCTX // GT
NT = NCTX // P
NCH = 4 * NT
H = 16
SCALE = float(1.0 / np.sqrt(np.float32(32.0)))
NEG = -1.0e30

C_L0Q, C_L0K, C_L1XQ, C_L1XK, C_L1AQ, C_L1AK = 0, 4, 8, 12, 16, 20
R_L0X, R_L0V, R_L0O, R_XV, R_XO, R_AV, R_AO = range(7)
BSLOT = [0, 1, 2, 3, 0, 1, 2]


CALLS = {
    "matmul": lambda e, a, k: e.matmul(*a, **k),
    "transpose": lambda e, a, k: e.transpose(*a, **k),
    "activation": lambda e, a, k: e.activation(*a, **k),
    "tensor_tensor": lambda e, a, k: e.tensor_tensor(*a, **k),
    "tensor_scalar": lambda e, a, k: e.tensor_scalar(*a, **k),
    "scalar_tensor_tensor": lambda e, a, k: e.scalar_tensor_tensor(*a, **k),
    "tensor_reduce": lambda e, a, k: e.tensor_reduce(*a, **k),
    "tensor_copy": lambda e, a, k: e.tensor_copy(*a, **k),
    "reciprocal": lambda e, a, k: e.reciprocal(*a, **k),
    "memset": lambda e, a, k: e.memset(*a, **k),
    "affine_select": lambda e, a, k: e.affine_select(*a, **k),
    "bn_stats": lambda e, a, k: e.bn_stats(*a, **k),
    "bn_aggr": lambda e, a, k: e.bn_aggr(*a, **k),
    "dma_start": lambda e, a, k: e.dma_start(*a, **k),
}


class Noted:


    def matmul(self, *a, **k):
        return "matmul", a, k

    def transpose(self, *a, **k):
        return "transpose", a, k

    def activation(self, *a, **k):
        return "activation", a, k

    def tensor_tensor(self, *a, **k):
        return "tensor_tensor", a, k

    def tensor_scalar(self, *a, **k):
        return "tensor_scalar", a, k

    def scalar_tensor_tensor(self, *a, **k):
        return "scalar_tensor_tensor", a, k

    def tensor_reduce(self, *a, **k):
        return "tensor_reduce", a, k

    def tensor_copy(self, *a, **k):
        return "tensor_copy", a, k

    def reciprocal(self, *a, **k):
        return "reciprocal", a, k

    def memset(self, *a, **k):
        return "memset", a, k

    def affine_select(self, *a, **k):
        return "affine_select", a, k

    def bn_stats(self, *a, **k):
        return "bn_stats", a, k

    def bn_aggr(self, *a, **k):
        return "bn_aggr", a, k

    def dma_start(self, *a, **k):
        return "dma_start", a, k


class Queues:

    def __init__(self):
        self.q = {e: [] for e in ("pe", "act", "dve", "pool", "sp")}
        self.n = {e: 0 for e in self.q}
        self.seen = {e: {} for e in self.q}
        self.chained = False

    def op(self, eng, fn, *waits, inc=True):
        waits = [w for w in waits if w is not None]
        if self.chained and eng in ("act", "dve", "pool") and self.n[eng]:
            waits.append((eng, self.n[eng]))
        need = []
        for s, v in waits:
            if self.seen[eng].get(s, 0) < v:
                self.seen[eng][s] = v
                need.append((s, v))
        if inc:
            self.n[eng] += 1
        self.q[eng].append((need, fn(Noted()), eng if inc else None, 1))
        return (eng, self.n[eng])

    def dma(self, fn, sem, *waits):
        need = []
        for s, v in [w for w in waits if w is not None]:
            if self.seen["sp"].get(s, 0) < v:
                self.seen["sp"][s] = v
                need.append((s, v))
        self.n[sem] = self.n.get(sem, 0) + 16
        self.q["sp"].append((need, fn(Noted()), sem, 16))
        return (sem, self.n[sem])

    def play(self, eng, e, sems):
        for need, (name, args, kw), sem, by in self.q[eng]:
            for s, v in need:
                e.wait_ge(sems[s], v)
            ins = CALLS[name](e, args, kw)
            if sem is not None:
                ins.then_inc(sems[sem], by)


def build(nc, a):
    K = Queues()
    op, dma = K.op, K.dma
    ctx = ExitStack()
    with ctx:
        def sb(name, shape, dt=F32):
            return ctx.enter_context(nc.sbuf_tensor(name, shape, dt))

        WKV = sb("WKV", [P, 4, NC, D], F32R)
        CTX = sb("CTX", [P, 2, 2, NC, GT], F32R)
        KHL = sb("KHL", [P, 2, 2, NC, GT], F32R)
        QB = sb("QB", [P, 2, NC, 4, 256], F32R)
        WB = sb("WB", [P, 13824])
        WA = sb("WA", [P, 8192])
        X = sb("X", [P, 2, D])
        XT = sb("XT", [P, NC, 256])
        BI = sb("BI", [P, 4, D])
        BC = sb("BC", [P, 24])
        ident = sb("ident", [P, P])
        mask0 = sb("mask0", [P, 384])
        mask1 = sb("mask1", [P, 256])
        lt = sb("lt", [P, 256])
        st = sb("st", [P, 2, 6])
        mv = sb("mv", [P, 2, 2])
        rstd = sb("rstd", [P, 2])
        half = sb("half", [P, 2])
        small = sb("small", [P, 1024])
        PB = ctx.enter_context(nc.psum_tensor("PB", [P, 8, 512], F32))

        def wb(o, n):
            return WB[:, o:o + n]

        def bank(b, o=0, n=512):
            return PB[:, b, o:o + n]

        K.chained = True
        m_x = dma(lambda e: e.dma_start(X[:, :, :], a["x"]), "d_x")
        m_wkv = dma(lambda e: e.dma_start(WA[:, 0:4096], a["wkv"]), "d_wa")
        m_bc = dma(lambda e: e.dma_start(BC[:, :], a["bcol"]), "d_bc")

        def load_bias(r, *w):
            s = BSLOT[r]
            return dma(lambda e: e.dma_start(BI[:, s, :], a["brow"][r:r + 1, :].to_broadcast([P, D])),
                       f"d_bi{s}", *w)

        m_bi = {r: load_bias(r) for r in (R_L0X, R_L0V, R_L0O, R_XV)}
        m_l0x = dma(lambda e: e.dma_start(wb(8192, 4096), a["l0x"]), "d_w0")

        op("pool", lambda e: e.memset(half[:, :], -0.5))
        op("pool", lambda e: e.memset(ident[:, :], 0.0))
        op("pool", lambda e: e.affine_select(out=ident[:, :], in_=ident[:, :], compare_op=ALU.not_equal,
                                             fill=1.0, base=0, pattern=[[-1, P]], channel_multiplier=1))
        op("pool", lambda e: e.memset(mask0[:, :], 0.0))
        op("pool", lambda e: e.affine_select(out=mask0[:, 0:128], in_=mask0[:, 0:128], compare_op=ALU.is_ge,
                                             fill=NEG, base=0, pattern=[[-1, P]], channel_multiplier=1))
        op("pool", lambda e: e.affine_select(out=mask0[:, 128:256], in_=mask0[:, 128:256], compare_op=ALU.is_ge,
                                             fill=NEG, base=-1, pattern=[[1, P]], channel_multiplier=-1))
        op("pool", lambda e: e.affine_select(out=mask0[:, 256:384], in_=mask0[:, 256:384], compare_op=ALU.is_ge,
                                             fill=NEG, base=0, pattern=[[-1, P]], channel_multiplier=1))
        op("pool", lambda e: e.memset(mask1[:, :], 0.0))
        for w in range(2):
            op("pool", lambda e, w=w: e.memset(mask1[0:64, 128 * w + 64:128 * w + 128], NEG))
            op("pool", lambda e, w=w: e.memset(mask1[64:128, 128 * w:128 * w + 64], NEG))
        op("pool", lambda e: e.memset(lt[:, :], 1.0))
        op("pool", lambda e: e.affine_select(out=lt[:, :].rearrange("p (a b) -> p a b", a=16),
                                             in_=lt[:, :].rearrange("p (a b) -> p a b", a=16),
                                             compare_op=ALU.is_gt, fill=0.0, base=0,
                                             pattern=[[1, 16], [-1, 16]], channel_multiplier=0))
        m_const = op("pool", lambda e: e.memset(QB[:, :, :, :, :].bitcast(F32), 0.0))
        wraw = WA[:, 0:4096].rearrange("p (m c n) -> p m c n", m=2, c=NC)
        for m in range(2):
            hi = op("act", lambda e, m=m: e.activation(WKV[:, 2 * m, :, :], wraw[:, m], ACT.Copy), m_wkv)
            m_wsplit = op("dve", lambda e, m=m: e.tensor_tensor(
                WKV[:, 2 * m + 1, :, :], wraw[:, m], WKV[:, 2 * m, :, :].bitcast(F32), ALU.subtract), m_wkv, hi)
        m_wl0 = dma(lambda e: e.dma_start(WA[:, :], a["l0a"]), "d_wa", m_wsplit)

        NP1 = NG // 2
        sums = small[:, 0:4 * NG]
        m_red = []
        for n in range(NP1):
            r = n % 4
            m = dma(lambda e, n=n, r=r: e.dma_start(
                wb(2048 * r, 2048).rearrange("p (g f) -> p g f", g=2),
                a["ctx"][2 * n:2 * n + 2].rearrange("g p f -> p g f")), f"d_c{r}",
                m_red[n - 4] if n >= 4 else None)
            m_red.append(op("dve", lambda e, n=n, r=r: e.tensor_reduce(
                sums[:, 8 * n:8 * n + 8], wb(2048 * r, 2048).rearrange("p (g f) -> p g f", f=GT),
                axis=AX.X, op=ALU.add), m))
        csum = small[:, 400:404]
        op("dve", lambda e: e.tensor_reduce(csum, sums.rearrange("p (g c) -> p c g", c=NC), axis=AX.X, op=ALU.add))
        SBC = wb(0, 512).rearrange("p (c i) -> p c i", c=NC)
        m_sbc = op("dve", lambda e: e.tensor_scalar(SBC, csum.unsqueeze(2).to_broadcast([P, NC, P]),
                                                    1.0 / NCTX, None, ALU.mult))

        def layernorm(XN, *w):
            for i in range(2):
                op("dve", lambda e, i=i: e.bn_stats(st[:, i, :], X[:, i, :]), *w)
                m = op("dve", lambda e, i=i: e.bn_aggr(mv[:, i, :], st[:, i, :]))
            op("pool", lambda e: e.tensor_scalar(rstd[:, :], mv[:, :, 1], 1e-5, None, ALU.add), m)
            m = op("pool", lambda e: e.tensor_tensor(rstd[:, :], rstd[:, :], half[:, :], ALU.pow))
            for i in range(2):
                m = op("dve", lambda e, i=i: e.tensor_scalar(
                    XN[:, i, :], X[:, i, :], mv[:, i, 0:1], rstd[:, i:i + 1], ALU.subtract, ALU.mult), m)
            return m

        def transpose_to(dst, src, m_src, *w, roll=0, unroll=0):
            for c in range(NC):
                for i in range(2):
                    m = op("pe", lambda e, c=c, i=i: e.transpose(
                        bank(c // 2, 256 * (c % 2) + 128 * i, 128), src[:, i, 128 * c:128 * c + 128], ident[:, :]),
                        m_src, m_const, *w, inc=(c % 2 == 1 and i == 1))
                if c % 2:
                    b = c // 2
                    d = dst[:, 2 * b:2 * b + 2, :]
                    s = bank(b).rearrange("p (c i) -> p c i", c=2)
                    if not roll:
                        out = op("act" if b else "dve", lambda e, d=d, s=s, b=b: (
                            e.activation(d, s, ACT.Copy) if b else e.tensor_copy(d, s)), m)
                    else:
                        op("dve", lambda e, d=d, s=s: e.tensor_copy(d[:, :, 0:256 - roll], s[:, :, roll:256]), m)
                        out = op("dve", lambda e, d=d, s=s: e.tensor_copy(d[:, :, 256 - roll:256], s[:, :, 0:roll]))
                    if not b:
                        first = out
            return [first, out]

        def last(eng):
            return (eng, K.n[eng])

        XN = wb(12288, 1024).rearrange("p (i n) -> p i n", i=2)
        m = layernorm(XN, m_x)
        m_xt = transpose_to(XT, XN, m)
        for i in range(2):
            m_xb = op("dve", lambda e, i=i: e.tensor_tensor(X[:, i, :], X[:, i, :], BI[:, 0, :], ALU.add), m_bi[R_L0X])
        w0 = wb(8192, 4096).rearrange("p (m c n) -> p m c n", m=2, c=NC)
        for i in range(2):
            for c in range(NC):
                op("pe", lambda e, i=i, c=c: e.matmul(bank(2 + i), XT[:, c, 128 * i:128 * i + 128], w0[:, 0, c, :],
                                                      start=(c == 0), stop=False), *m_xt, m_l0x, inc=False)
            for c in range(NC):
                m = op("pe", lambda e, i=i, c=c: e.matmul(bank(2 + i), SBC[:, c, :], w0[:, 1, c, :],
                                                          start=False, stop=(c == NC - 1)), m_sbc, inc=(c == NC - 1))
            m_xr = op("dve", lambda e, i=i: e.tensor_tensor(X[:, i, :], X[:, i, :], bank(2 + i), ALU.add), m)
        m_bi[R_XO] = load_bias(R_XO, m_xb)

        def self_attention(cq, ck, rv, ro, m_w, mask, blocks, roll):
            NB = len(blocks)
            W = 128 * NB
            XN = wb(9728, 1024).rearrange("p (i n) -> p i n", i=2)
            QT = wb(0, 1024).rearrange("p (c i) -> p c i", c=NC)
            KT = wb(1024, 1024).rearrange("p (c i) -> p c i", c=NC)
            V = wb(2048, 1024).rearrange("p (i n) -> p i n", i=2)
            SM = wb(3072, 2 * 4 * W).rearrange("p (b s w) -> p b s w", b=2, s=4)
            PT = wb(6144, 4 * W).rearrange("p (s w) -> p s w", s=4)
            AT = wb(7680, 1024).rearrange("p (i n) -> p i n", i=2)
            ATT = wb(8704, 1024).rearrange("p (c i) -> p c i", c=NC)
            wq = WA[:, 0:6144].rearrange("p (c n) -> p c n", c=NC)
            wo = WA[:, 6144:8192].rearrange("p (c n) -> p c n", c=NC)
            nm = small[:, 0:8].rearrange("p (s i) -> p s i", i=2)
            su = small[:, 16:48].rearrange("p (h i) -> p h i", i=2)
            rc = small[:, 48:80].rearrange("p (h i) -> p h i", i=2)
            m = layernorm(XN, last("pe"))
            m_xt = transpose_to(XT, XN, m, roll=roll)
            for m8 in range(8):
                b = 2 + m8 // 2
                o = 256 * (m8 % 2)
                for c in range(NC):
                    m = op("pe", lambda e, m8=m8, c=c, b=b, o=o: e.matmul(
                        bank(b, o, 256), wq[:, c, 128 * m8:128 * m8 + 128], XT[:, c, :],
                        start=(c == 0), stop=(c == NC - 1)), *m_xt, m_w, inc=(c == NC - 1))
                if m8 % 2:
                    for z in (m8 - 1, m8):
                        oz = 256 * (z % 2)
                        if z < 4:
                            m_q = op("dve", lambda e, z=z, b=b, oz=oz: e.tensor_scalar(
                                QT[:, z, :], bank(b, oz, 256), BC[:, cq + z:cq + z + 1], SCALE, ALU.add, ALU.mult),
                                m, m_bc)
                        else:
                            m_q = op("dve", lambda e, z=z, b=b, oz=oz: e.tensor_scalar(
                                KT[:, z - 4, :], bank(b, oz, 256), BC[:, ck + z - 4:ck + z - 3], None, ALU.add),
                                m, m_bc)
            for i in range(2):
                for c in range(NC):
                    m = op("pe", lambda e, i=i, c=c: e.matmul(
                        bank(6 + i), XT[:, c, 128 * i:128 * i + 128], wq[:, c, 1024:1536],
                        start=(c == 0), stop=(c == NC - 1)), inc=(c == NC - 1))
                m_v = op("dve", lambda e, i=i: e.tensor_tensor(V[:, i, :], bank(6 + i), BI[:, BSLOT[rv], :], ALU.add),
                         m, m_bi[rv])
            for i in range(2):
                m_xb = op("dve", lambda e, i=i: e.tensor_tensor(X[:, i, :], X[:, i, :], BI[:, BSLOT[ro], :], ALU.add),
                          m_bi[ro])
            m_sm, m_tr, m_pt = {}, {}, {}
            rng = {i: [z for z, (q, _) in enumerate(blocks) if q == i] for i in range(2)}
            m_ex = {}

            def scores(c):
                for s in range(4):
                    for i in range(2):
                        z0, nz = rng[i][0], len(rng[i])
                        j0 = blocks[z0][1]
                        m = op("pe", lambda e, s=s, i=i, z0=z0, nz=nz, j0=j0: e.matmul(
                            bank(s, 128 * z0, 128 * nz), QT[32 * s:32 * s + 32, c, 128 * i:128 * i + 128],
                            KT[32 * s:32 * s + 32, c, 128 * j0:128 * (j0 + nz)], start=True, stop=True),
                            m_q, m_sm.get(c - 1), inc=(s == 3 and i == 1))
                b = c % 2
                m_sm[c] = op("dve", lambda e: e.tensor_tensor(
                    SM[:, b], PB[:, 0:4, 0:W], mask[:, 0:W].unsqueeze(1).to_broadcast([P, 4, W]), ALU.add),
                    m, m_tr.get(c - 2))
                for i in range(2):
                    z0, nz = rng[i][0], len(rng[i])
                    m = op("dve", lambda e, i=i, z0=z0, nz=nz: e.tensor_reduce(
                        nm[:, :, i], SM[:, b, :, 128 * z0:128 * (z0 + nz)], axis=AX.X, op=ALU.max, negate=True),
                        m_ex.get(c - 1))
                for s in range(4):
                    for i in range(2):
                        z0, nz = rng[i][0], len(rng[i])
                        v = SM[:, b, s, 128 * z0:128 * (z0 + nz)]
                        m_ex[c] = op("act", lambda e, s=s, i=i, v=v: e.activation(
                            v, v, ACT.Exp, bias=nm[:, s, i:i + 1], accum_out=su[:, 4 * c + s, i:i + 1]), m)

            def mix(c):
                for s in range(4):
                    pb = 4 + s % 2
                    for z in range(NB):
                        m = op("pe", lambda e, s=s, z=z, pb=pb: e.transpose(
                            bank(pb, 128 * z, 128), SM[:, c % 2, s, 128 * z:128 * z + 128], ident[:, :]),
                            m_ex[c], m_pt.get(4 * c + s - 2), inc=(z == NB - 1))
                    m_tr[c] = m
                    m_pt[4 * c + s] = op("dve", lambda e, s=s, pb=pb: e.tensor_copy(
                        PT[:, s, :], bank(pb, 0, W)), m, m_pvs.get(4 * c + s - 4))
                    h = 4 * c + s
                    for z, (i, j) in enumerate(blocks):
                        m_pvs[h] = op("pe", lambda e, s=s, h=h, z=z, i=i, j=j: e.matmul(
                            bank(6 + i, 32 * h, 32), PT[:, s, 128 * z:128 * z + 128], V[:, j, 32 * h:32 * h + 32],
                            start=(z == rng[i][0]), stop=(z == rng[i][-1])), m_pt[4 * c + s], m_v, inc=(z == NB - 1))

            m_pvs = {}
            scores(0)
            for c in range(NC):
                if c + 1 < NC:
                    scores(c + 1)
                mix(c)
            m = op("dve", lambda e: e.reciprocal(rc, su), m_ex[3])
            for i in range(2):
                m = op("dve", lambda e, i=i: e.tensor_tensor(
                    AT[:, i, :].rearrange("p (h d) -> p h d", h=H), bank(6 + i).rearrange("p (h d) -> p h d", h=H),
                    rc[:, :, i].unsqueeze(2).to_broadcast([P, H, 32]), ALU.mult), m_pvs[15])
            m_at = transpose_to(ATT, AT, m, m_sm[3], roll=(256 - roll) % 256)
            for i in range(2):
                for c in range(NC):
                    m = op("pe", lambda e, i=i, c=c: e.matmul(
                        bank(2 + i), ATT[:, c, 128 * i:128 * i + 128], wo[:, c, :],
                        start=(c == 0), stop=(c == NC - 1)), *m_at, inc=(c == NC - 1))
                op("dve", lambda e, i=i: e.tensor_tensor(X[:, i, :], X[:, i, :], bank(2 + i), ALU.add), m)
            return m_xb

        m_xb = self_attention(C_L0Q, C_L0K, R_L0V, R_L0O, m_wl0, mask0, [(0, 0), (1, 0), (1, 1)], 0)
        m_bi[R_AV] = load_bias(R_AV, m_xb)
        m_bi[R_AO] = load_bias(R_AO, m_xb)
        m_wl1 = dma(lambda e: e.dma_start(WA[:, :], a["l1a"]), "d_wa", last("pe"))

        def ranks(dst, v, E, tmp, n=1):
            g = tmp.rearrange("p (g a b) -> p g a b", g=n, a=E)
            t = small[:, 512:512 + n * E * E].rearrange("p (g a b) -> p g a b", g=n, a=E)
            for x in range(n):
                vv = v[:, x * E:(x + 1) * E]
                o = vv.unsqueeze(1).to_broadcast([P, E, E])
                s = vv.unsqueeze(2).to_broadcast([P, E, E])
                l = lt[:, :].rearrange("p (a b) -> p a b", a=16)[:, 0:E, 0:E]
                op("dve", lambda e, x=x, o=o, s=s: e.tensor_tensor(g[:, x], o, s, ALU.is_equal))
                op("dve", lambda e, x=x, l=l: e.tensor_tensor(g[:, x], g[:, x], l, ALU.mult), m_const)
                op("dve", lambda e, x=x, o=o, s=s: e.tensor_tensor(t[:, x], o, s, ALU.is_gt))
                op("dve", lambda e, x=x: e.tensor_tensor(g[:, x], g[:, x], t[:, x], ALU.add))
                op("dve", lambda e, x=x: e.tensor_reduce(dst[:, x * E:(x + 1) * E], g[:, x], axis=AX.X, op=ALU.add))

        XNF = wb(12544, 1024).rearrange("p (i n) -> p i n", i=2)
        gw = small[:, 0:64].rearrange("p (c n) -> p c n", c=NC)
        m = layernorm(XNF, last("pe"))
        gb = small[:, 64:80]
        m_gw = dma(lambda e: e.dma_start(small[:, 0:80], a["l0g"]), "d_g", last("dve"), last("act"))
        m_xt = transpose_to(XT, XNF, m)
        comb = small[:, 80:112].rearrange("p (i n) -> p i n", i=2)
        sc, v, rk, t16 = small[:, 112:128], small[:, 128:144], small[:, 144:160], small[:, 160:176]
        gs, gm, t1 = small[:, 176:180], small[:, 180:184], small[:, 184:185]
        tmp = small[:, 768:1024]
        for i in range(2):
            for c in range(NC):
                m = op("pe", lambda e, i=i, c=c: e.matmul(bank(3, 16 * i, 16), XT[:, c, 128 * i:128 * i + 128],
                                                          gw[:, c, :], start=(c == 0), stop=(c == NC - 1)),
                       *m_xt, m_gw, inc=(c == NC - 1))
        m_gate = m
        for i in range(2):
            m = op("act", lambda e, i=i: e.activation(sc, bank(3, 16 * i, 16), ACT.Sigmoid), m_gate, last("dve"))
            op("dve", lambda e: e.tensor_tensor(v, sc, gb, ALU.add), m)
            ranks(rk, v, 4, tmp[:, 0:64], n=4)
            op("dve", lambda e: e.tensor_scalar(t16, rk, 2.0, None, ALU.is_lt))
            op("dve", lambda e: e.tensor_tensor(t16, t16, v, ALU.mult))
            op("dve", lambda e: e.tensor_reduce(gs, t16.rearrange("p (g a) -> p g a", g=4), axis=AX.X, op=ALU.add))
            ranks(gm, gs, 4, tmp[:, 0:16])
            op("dve", lambda e: e.tensor_scalar(gm, gm, 2.0, None, ALU.is_lt))
            gmb = gm.unsqueeze(2).to_broadcast([P, 4, 4])
            v4 = v.rearrange("p (g a) -> p g a", g=4)
            t4 = t16.rearrange("p (g a) -> p g a", g=4)
            op("dve", lambda e: e.tensor_tensor(v4, v4, gmb, ALU.mult))
            op("dve", lambda e: e.tensor_scalar(t4, gmb, -1.0, 1.0e30, ALU.add, ALU.mult))
            op("dve", lambda e: e.tensor_tensor(v, v, t16, ALU.add))
            ranks(rk, v, 16, tmp)
            op("dve", lambda e: e.tensor_scalar(t16, rk, 4.0, None, ALU.is_lt))
            op("dve", lambda e: e.tensor_tensor(t16, t16, sc, ALU.mult))
            op("dve", lambda e: e.tensor_reduce(t1, t16, axis=AX.X, op=ALU.add))
            op("dve", lambda e: e.tensor_scalar(t1, t1, 1e-20, None, ALU.add))
            op("dve", lambda e: e.reciprocal(t1, t1))
            op("dve", lambda e, i=i: e.tensor_scalar(comb[:, i, :], t16, t1, 2.5, ALU.mult, ALU.mult))
        ring = lambda r: wb(4608 * r, 4608).rearrange("p (m f) -> p m f", m=3)
        hT = wb(10240, 1536).rearrange("p (r k i) -> p r k i", r=2, k=3)
        sg = wb(11776, 768).rearrange("p (k i) -> p k i", k=3)
        m_free, m_y, m_acc, m_h = {}, {}, {}, {}
        m_start = [last("pe"), last("dve"), last("act")]
        K.chained = False

        def up0(x):
            r = x % 2
            m_w = dma(lambda e, x=x, r=r: e.dma_start(wb(4608 * r, 4608), a["l0f"][x]), f"d_f{r}",
                      m_free.get(x - 2), *m_start)
            w1 = ring(r)[:, 0, :].rearrange("p (c n) -> p c n", c=NC)
            w3 = ring(r)[:, 1, :].rearrange("p (c n) -> p c n", c=NC)
            for k in range(3):
                n = 3 * x + k
                for u, w in enumerate((w1, w3)):
                    for c in range(NC):
                        m = op("pe", lambda e, u=u, w=w, c=c, k=k: e.matmul(
                            bank(k, 256 * u, 256), w[:, c, 128 * k:128 * k + 128], XT[:, c, :],
                            start=(c == 0), stop=(c == NC - 1)), m_w, m_h.get(n - 3), inc=(u == 1 and c == NC - 1))
                ms = op("act", lambda e, k=k: e.activation(sg[:, k, :], bank(k, 0, 256), ACT.Silu), m, m_h.get(n - 3),
                        *m_start)
                m_h[n] = op("dve", lambda e, k=k, r=r: e.tensor_tensor(
                    hT[:, r, k, :], sg[:, k, :], bank(k, 256, 256), ALU.mult), ms, m_free.get(x - 2))

        def down0(x):
            r = x % 2
            w2 = ring(r)[:, 2, :].rearrange("p (k n) -> p k n", k=3)
            for i in range(2):
                b = 4 + 2 * r + i
                for k in range(3):
                    m = op("pe", lambda e, i=i, k=k, b=b, r=r, w2=w2: e.matmul(
                        bank(b), hT[:, r, k, 128 * i:128 * i + 128], w2[:, k, :], start=(k == 0), stop=(k == 2)),
                        m_h[3 * x + k], m_acc.get((x - 2, i)), inc=(k == 2))
                s = comb[:, i, x:x + 1] if x < 16 else 1.0
                m_acc[x, i] = op("dve", lambda e, i=i, b=b, s=s: e.scalar_tensor_tensor(
                    out=X[:, i, :], in0=bank(b), scalar=s, in1=X[:, i, :], op0=ALU.mult, op1=ALU.add),
                    m, m_acc.get((x - 1, i)), *m_start)
            m_free[x] = m

        for x in range(17):
            up0(x)
            if x:
                down0(x - 1)
        down0(16)
        K.chained = True

        raw = lambda r: wb(1024 * r, 1024)
        V = wb(3072, 1024).rearrange("p (b n) -> p b n", b=2)
        VS = wb(4096, 512).rearrange("p (b n) -> p b n", b=4)
        EE = wb(4608, 4096).rearrange("p (b s i) -> p b s i", b=4, s=4)
        OT = wb(8704, 1024).rearrange("p (c i) -> p c i", c=NC)
        wq = wb(9728, 2048).rearrange("p (c n) -> p c n", c=NC)
        wo = wb(11776, 2048).rearrange("p (c n) -> p c n", c=NC)
        XNX = wb(4608, 1024).rearrange("p (i n) -> p i n", i=2)
        m_end = [last("pe"), last("dve"), last("act")]
        m_wx = dma(lambda e: e.dma_start(wb(9728, 4096), a["l1x"]), "d_w0", *m_end)
        m_raw, m_lo = {}, {}

        def load_ctx(g):
            m_raw[g] = dma(lambda e: e.dma_start(raw(g % 3), a["ctx"][g]), f"d_c{g % 3}", m_lo.get(g - 3), *m_end)

        for g in range(3):
            load_ctx(g)
        m = layernorm(XNX, *m_end)
        m_xt = transpose_to(XT, XNX, m)
        qf = OT
        for c4 in range(NC):
            for c in range(NC):
                m = op("pe", lambda e, c=c, c4=c4: e.matmul(
                    bank(2 + c4, 0, 256), wq[:, c, 128 * c4:128 * c4 + 128], XT[:, c, :],
                    start=(c == 0), stop=(c == NC - 1)), *m_xt, m_wx, inc=(c == NC - 1))
            op("dve", lambda e, c4=c4: e.tensor_scalar(
                qf[:, c4, :], bank(2 + c4, 0, 256), BC[:, C_L1XQ + c4:C_L1XQ + c4 + 1], SCALE, ALU.add, ALU.mult), m)
            for s in range(4):
                q = slice(32 * s, 32 * s + 32)
                op("dve", lambda e, c4=c4, s=s, q=q: e.tensor_copy(QB[q, 0, c4, s, :], qf[q, c4, :]), m_const)
                m_q = op("dve", lambda e, c4=c4, s=s, q=q: e.tensor_tensor(
                    QB[q, 1, c4, s, :], qf[q, c4, :], QB[q, 0, c4, s, :].bitcast(F32), ALU.subtract))
        for i in range(2):
            op("dve", lambda e, i=i: e.tensor_tensor(X[:, i, :], X[:, i, :], BI[:, BSLOT[R_XO], :], ALU.add),
               m_bi[R_XO])
        m_pro = last("dve")
        K.chained = False

        nm = small[:, 0:16].rearrange("p (b s) -> p b s", b=4)
        su = small[:, 16:32].rearrange("p (b s) -> p b s", b=4)
        rc = small[:, 32:48].rearrange("p (b s) -> p b s", b=4)
        m_khi, m_klo, m_kp, m_vp, m_vev, m_vs, m_ex, m_mx, m_rc, m_pv, m_s = ({} for _ in range(11))

        def split_ctx(g):
            b = g % 2
            hi = op("dve", lambda e: e.tensor_copy(CTX[:, b, 0, :, :].rearrange("p c j -> p (c j)"), raw(g % 3)),
                    m_raw[g], m_vp.get(2 * (g - 2) + 1), m_kp.get((g - 2, 3)))
            m_lo[g] = op("pool", lambda e: e.tensor_tensor(
                CTX[:, b, 1, :, :].rearrange("p c j -> p (c j)"), raw(g % 3),
                CTX[:, b, 0, :, :].rearrange("p c j -> p (c j)").bitcast(F32), ALU.subtract), hi)
            if g + 3 < NG:
                load_ctx(g + 3)

        def project_k(g, ch):
            b = g % 2
            n = 0
            for wh, xh in ((0, 0), (0, 1), (1, 0)):
                for c in range(NC):
                    n += 1
                    m = op("pe", lambda e, wh=wh, xh=xh, c=c, n=n: e.matmul(
                        bank(4, 0, GT), WKV[:, wh, c, 128 * ch:128 * ch + 128], CTX[:, b, xh, c, :],
                        start=(n == 1), stop=(n == 12)), m_lo[g], m_klo.get(m_kprev[0]), inc=(n == 12))
            m_kp[g, ch] = m
            m_kprev[0] = (g, ch)

        m_kprev = [None]

        def evac_k_hi(g, ch):
            m_khi[g, ch] = op("act", lambda e: e.activation(
                KHL[:, g % 2, 0, ch, :], bank(4, 0, GT), ACT.Identity, bias=BC[:, C_L1XK + ch:C_L1XK + ch + 1]),
                m_kp[g, ch])

        def evac_k_lo(g, ch):
            m_klo[g, ch] = op("dve", lambda e: e.scalar_tensor_tensor(
                out=KHL[:, g % 2, 1, ch, :], in0=bank(4, 0, GT), scalar=BC[:, C_L1XK + ch:C_L1XK + ch + 1],
                in1=KHL[:, g % 2, 0, ch, :].bitcast(F32), op0=ALU.add, op1=ALU.subtract), m_khi[g, ch])

        def project_v(t, half):
            g, b, j = t // 2, (t // 2) % 2, 128 * (t % 2)
            steps = [(xh, wh, c) for xh, wh in ((0, 0), (0, 1), (1, 0)) for c in range(NC)]
            for n in range(6 * half, 6 * half + 6):
                xh, wh, c = steps[n]
                m = op("pe", lambda e, xh=xh, wh=wh, c=c, n=n: e.matmul(
                    bank(5), CTX[:, b, xh, c, j:j + 128], WKV[:, 2 + wh, c, :],
                    start=(n == 0), stop=(n == 11)), m_lo[g], m_vev.get(t - 1), inc=(n == 11))
            if half:
                m_vp[t] = m

        def evac_v(t):
            m_vev[t] = op("dve", lambda e: e.tensor_tensor(V[:, t % 2, :], bank(5), BI[:, BSLOT[R_XV], :], ALU.add),
                          m_vp[t], m_vs.get(4 * (t - 2) + 3), m_bi[R_XV])

        def scores(k):
            t, c = k // 4, k % 4
            g, b, j = t // 2, (t // 2) % 2, 128 * (t % 2)
            for s in range(4):
                o = bank(2 * (k % 2) + s // 2, 256 * (s % 2), 256)
                for n, (kh, qh) in enumerate(((0, 0), (0, 1), (1, 0))):
                    m = op("pe", lambda e, o=o, kh=kh, qh=qh, s=s, n=n: e.matmul(
                        o, KHL[:, b, kh, c, j:j + 128], QB[:, qh, c, s, :], start=(n == 0), stop=(n == 2)),
                        m_klo[g, c], m_ex.get(k - 2), m_pro, inc=(s == 3 and n == 2))
            m_s[k] = m

        def softmax(k):
            b = k % 4
            pb = 2 * (k % 2)
            m_mx[k] = op("dve", lambda e: e.tensor_reduce(
                nm[:, b, :].rearrange("p (a s) -> p a s", a=2),
                PB[:, pb:pb + 2, :].rearrange("p a (s i) -> p a s i", s=2), axis=AX.X, op=ALU.max, negate=True),
                m_s[k], m_ex.get(k - 4))
            for s in range(4):
                m = op("act", lambda e, s=s: e.activation(
                    EE[:, b, s, :], bank(pb + s // 2, 256 * (s % 2), 256), ACT.Exp, bias=nm[:, b, s:s + 1],
                    accum_out=su[:, b, s:s + 1]), m_mx[k], m_pv.get(k - 4), m_rc.get(k - 4), inc=(s == 3))
            m_ex[k] = m

        def scale_v(k):
            b, t, c = k % 4, k // 4, k % 4
            m_rc[k] = op("dve", lambda e: e.reciprocal(rc[:, b, :], su[:, b, :]), m_ex[k], m_vs.get(k - 4))
            m_vs[k] = op("pool", lambda e: e.tensor_tensor(
                VS[:, b, :].rearrange("p (s d) -> p s d", s=4),
                V[:, t % 2, 128 * c:128 * c + 128].rearrange("p (s d) -> p s d", s=4),
                rc[:, b, :].unsqueeze(2).to_broadcast([P, 4, 32]), ALU.mult), m_rc[k], m_pv.get(k - 4), m_vev[t])

        def mix(k):
            t, c, b = k // 4, k % 4, k % 4
            for s in range(4):
                m = op("pe", lambda e, s=s: e.matmul(
                    PB[32 * s:32 * s + 32, 6 + c // 2, 256 * (c % 2):256 * (c % 2) + 256],
                    VS[:, b, 32 * s:32 * s + 32], EE[:, b, s, :],
                    start=(t == 0 and c % 2 == 0), stop=(t == NT - 1), skip_group_check=True),
                    m_vs[k], m_ex[k], inc=(s == 3))
            m_pv[k] = m

        split_ctx(0)
        for ch in range(4):
            project_k(0, ch)
            evac_k_hi(0, ch)
            evac_k_lo(0, ch)
        project_v(0, 0)
        project_v(0, 1)
        evac_v(0)
        split_ctx(1)
        lo_due = []
        for k in range(NCH):
            t, c = k // 4, k % 4
            g, tt = t // 2, t % 2
            scores(k)
            softmax(k)
            if k >= 1:
                scale_v(k - 1)
            for due in lo_due:
                evac_k_lo(*due)
            lo_due = []
            if c % 2 == 0:
                if g + 1 < NG:
                    ch = 2 * tt + c // 2
                    project_k(g + 1, ch)
                    evac_k_hi(g + 1, ch)
                    lo_due.append((g + 1, ch))
            elif t + 1 < NT:
                project_v(t + 1, c // 2)
                if c == 3:
                    evac_v(t + 1)
                    if tt == 0 and g + 2 < NG:
                        split_ctx(g + 2)
            if k >= 2:
                mix(k - 2)
        scale_v(NCH - 1)
        mix(NCH - 2)
        mix(NCH - 1)
        K.chained = True
        m = m_pv[NCH - 1]
        for b in range(2):
            m2 = op("act" if b else "dve", lambda e, b=b: (
                e.activation(OT[:, 2 * b:2 * b + 2, :].rearrange("p c i -> p (c i)"), bank(6 + b), ACT.Copy) if b
                else e.tensor_copy(OT[:, 0:2, :].rearrange("p c i -> p (c i)"), bank(6))), m)
        m1 = last("dve")
        for i in range(2):
            for c in range(NC):
                m = op("pe", lambda e, i=i, c=c: e.matmul(
                    bank(2 + i), OT[:, c, 128 * i:128 * i + 128], wo[:, c, :],
                    start=(c == 0), stop=(c == NC - 1)), m1, m2, m_wx, m_ex[NCH - 1], inc=(c == NC - 1))
            op("dve", lambda e, i=i: e.tensor_tensor(X[:, i, :], X[:, i, :], bank(2 + i), ALU.add), m)

        self_attention(C_L1AQ, C_L1AK, R_AV, R_AO, m_wl1, mask1, [(0, 0), (1, 1)], 64)

        m_end = [last("pe"), last("dve"), last("act")]
        XNM = WA[:, 0:1024].rearrange("p (i n) -> p i n", i=2)
        lng, lnb = WA[:, 1024:1536], WA[:, 1536:2048]
        b2 = WA[0:8, 2048:2560]
        b1 = WA[:, 2560:2688]
        gw = WA[:, 2688:2720].rearrange("p (c n) -> p c n", c=NC)
        gbb = WA[:, 2720:2728]
        pT = WA[0:8, 2816:3072].rearrange("p (i n) -> p i n", i=2)
        m_ln = dma(lambda e: e.dma_start(WA[:, 1024:2048].rearrange("p (a n) -> p a n", a=2),
                                         a["lngb"].unsqueeze(0).to_broadcast([P, 2, D])), "d_w0", *m_end)
        m_b2 = dma(lambda e: e.dma_start(b2, a["b2"]), "d_x", *m_end)
        m_b1 = dma(lambda e: e.dma_start(WA[:, 2560:2728], a["l1g"]), "d_g", *m_end)
        m_wf = {}
        m_done = {}
        NPC = 32

        def load_piece(n):
            m_wf[n] = dma(lambda e: e.dma_start(wb(4096 * (n % 3), 4096), a["l1f"][n]), f"d_f{n % 3}",
                          m_done.get(n - 3), *m_end)

        for n in range(3):
            load_piece(n)
        m = layernorm(XNM, *m_end)
        m_xt = transpose_to(XT, XNM, m)
        for i in range(2):
            for c in range(NC):
                m = op("pe", lambda e, i=i, c=c: e.matmul(bank(3, 8 * i, 8), XT[:, c, 128 * i:128 * i + 128],
                                                          gw[:, c, :], start=(c == 0), stop=(c == NC - 1)),
                       *m_xt, m_b1, inc=(c == NC - 1))
        comb = small[:, 80:96].rearrange("p (i n) -> p i n", i=2)
        lg, rk, t8, mxv, sv = small[:, 112:120], small[:, 120:128], small[:, 128:136], small[:, 136:137], small[:, 137:138]
        m_gate = m
        for i in range(2):
            op("dve", lambda e, i=i: e.tensor_tensor(lg, bank(3, 8 * i, 8), gbb, ALU.add), m_gate, last("act"))
            op("dve", lambda e: e.tensor_scalar(lg, lg, 1.0 / 0.9, None, ALU.mult))
            ranks(rk, lg, 8, tmp[:, 0:64])
            m = op("dve", lambda e: e.tensor_reduce(mxv, lg, axis=AX.X, op=ALU.max, negate=True))
            m = op("act", lambda e: e.activation(t8, lg, ACT.Exp, bias=mxv), m)
            op("dve", lambda e: e.tensor_scalar(rk, rk, 2.0, None, ALU.is_lt))
            op("dve", lambda e: e.tensor_tensor(t8, t8, rk, ALU.mult), m)
            op("dve", lambda e: e.tensor_reduce(sv, t8, axis=AX.X, op=ALU.add))
            op("dve", lambda e: e.reciprocal(sv, sv))
            m_cb = op("dve", lambda e, i=i: e.tensor_scalar(comb[:, i, :], t8, sv, None, ALU.mult))
        ACC = WA[:, 3072:4096].rearrange("p (i n) -> p i n", i=2)
        for i in range(2):
            m = op("pe", lambda e, i=i: e.transpose(PB[0:8, 2, 128 * i:128 * i + 128], comb[:, i, :], ident[:, :]), m_cb)
        m = op("dve", lambda e: e.tensor_copy(pT, PB[0:8, 2, 0:256].rearrange("p (i n) -> p i n", i=2)), m)
        for i in range(2):
            m2 = op("pe", lambda e, i=i: e.matmul(bank(4 + i), pT[:, i, :], b2, start=True, stop=True), m, m_b2)
            op("dve", lambda e, i=i: e.tensor_copy(ACC[:, i, :], bank(4 + i)), m2, *m_end)
        hT = wb(12288, 1024).rearrange("p (r i) -> p r i", r=4)
        m_start = [last("dve")]
        K.chained = False
        m_g, m_dn, m_acc = {}, {}, {}

        def up1(n):
            pc, f = n // 4, n % 4
            e_ = n // 16
            w1 = wb(4096 * (pc % 3), 2048).rearrange("p (c n) -> p c n", c=NC)
            for c in range(NC):
                m = op("pe", lambda e, c=c, f=f, n=n, w1=w1: e.matmul(
                    bank(n % 4, 0, 256), w1[:, c, 128 * f:128 * f + 128], XT[:, c, :],
                    start=(c == 0), stop=(c == NC - 1)), m_wf[pc], m_g.get(n - 4), *m_start, inc=(c == NC - 1))
            m_g[n] = op("act", lambda e, n=n: e.activation(
                hT[:, n % 4, :], bank(n % 4, 0, 256), ACT.Gelu, bias=b1[:, n:n + 1]), m, m_dn.get(n - 4), *m_start)

        def down1(n):
            pc, f = n // 4, n % 4
            e_, fc = n // 16, n % 16
            w2 = wb(4096 * (pc % 3) + 2048, 2048).rearrange("p (f n) -> p f n", f=4)
            for i in range(2):
                b = 4 + 2 * (e_ % 2) + i
                m = op("pe", lambda e, i=i, f=f, n=n, w2=w2, b=b: e.matmul(
                    bank(b), hT[:, n % 4, 128 * i:128 * i + 128], w2[:, f, :], start=(fc == 0), stop=(fc == 15)),
                    m_g[n], m_acc.get((e_ - 2, i)), inc=(i == 1))
            m_dn[n] = m
            if f == 3:
                m_done[pc] = m
                if pc + 3 < NPC:
                    load_piece(pc + 3)
            if fc == 15:
                for i in range(2):
                    b = 4 + 2 * (e_ % 2) + i
                    m_acc[e_, i] = op("dve", lambda e, i=i, b=b, e_=e_: e.scalar_tensor_tensor(
                        out=ACC[:, i, :], in0=bank(b), scalar=comb[:, i, e_:e_ + 1], in1=ACC[:, i, :],
                        op0=ALU.mult, op1=ALU.add), m, m_acc.get((e_ - 1, i)), *m_start)

        for n in range(128):
            up1(n)
            if n >= 2:
                down1(n - 2)
        down1(126)
        down1(127)
        K.chained = True
        for i in range(2):
            op("dve", lambda e, i=i: e.bn_stats(st[:, i, :], ACC[:, i, :]))
            m = op("dve", lambda e, i=i: e.bn_aggr(mv[:, i, :], st[:, i, :]))
        op("pool", lambda e: e.tensor_scalar(rstd[:, :], mv[:, :, 1], 1e-5, None, ALU.add), m)
        m = op("pool", lambda e: e.tensor_tensor(rstd[:, :], rstd[:, :], half[:, :], ALU.pow))
        for i in range(2):
            op("dve", lambda e, i=i: e.tensor_scalar(
                ACC[:, i, :], ACC[:, i, :], mv[:, i, 0:1], rstd[:, i:i + 1], ALU.subtract, ALU.mult), m)
            op("dve", lambda e, i=i: e.tensor_tensor(ACC[:, i, :], ACC[:, i, :], lng, ALU.mult), m_ln)
            op("dve", lambda e, i=i: e.tensor_tensor(ACC[:, i, :], ACC[:, i, :], lnb, ALU.add))
            m2 = op("dve", lambda e, i=i: e.tensor_tensor(X[:, i, :], X[:, i, :], ACC[:, i, :], ALU.add))
        m_out = dma(lambda e: e.dma_start(a["out"], X[:, :, :]), "d_out", m2)

        sems = {}
        for s in K.n:
            if s != "sp":
                sems[s] = ctx.enter_context(nc.semaphore("s_" + s))
        block = ctx.enter_context(nc.Block())

        @block.sync
        def _(e):
            K.play("sp", e, sems)
            e.wait_ge(sems["d_out"], m_out[1])

        @block.tensor
        def _(e):
            K.play("pe", e, sems)

        @block.scalar
        def _(e):
            K.play("act", e, sems)

        @block.vector
        def _(e):
            K.play("dve", e, sems)

        @block.gpsimd
        def _(e):
            K.play("pool", e, sems)


def layout(inp):
    f = {k: np.asarray(v) for k, v in inp.items()}

    def rows(w):
        return w.reshape(-1, P, w.shape[-1]).transpose(1, 0, 2)

    def cols(v):
        return v.reshape(-1, P).T

    def flat(*parts):
        return np.ascontiguousarray(np.concatenate([p.reshape(P, -1) for p in parts], axis=1))

    def rep(v):
        return np.broadcast_to(v.reshape(1, -1), (P, v.size))

    ctx = f["ctx_1024"].reshape(NG, GT, NC, P).transpose(0, 3, 2, 1).reshape(NG, P, NC * GT)
    w = f["L0_xattn_W"]
    qkv = f["L1_attn_w_qkv"].reshape(D, H, 3, 32).transpose(0, 2, 1, 3).reshape(D, 3 * D)
    bq = f["L1_attn_b_qkv"].reshape(H, 3, 32).transpose(1, 0, 2).reshape(3, D)
    b0 = f["L0_attn_bqkv"].reshape(3, D)
    w1 = np.concatenate([f["L0_ffn_w1"], f["L0_ffn_ws1"][None]])
    w2 = np.concatenate([f["L0_ffn_w2"], f["L0_ffn_ws2"][None]])
    w3 = np.concatenate([f["L0_ffn_w3"], f["L0_ffn_ws3"][None]])
    l0f = np.stack([flat(rows(w1[e].T), rows(w3[e].T), rows(w2[e].T)) for e in range(17)])
    l1f = []
    for e in range(8):
        for q in range(4):
            l1f.append(flat(rows(f["L1_ffn_w1"][e][:, 512 * q:512 * q + 512]),
                            rows(f["L1_ffn_w2"][e][512 * q:512 * q + 512])))
    return {
        "x": np.ascontiguousarray(f["x"].reshape(2, P, D).transpose(1, 0, 2)),
        "ctx": np.ascontiguousarray(ctx),
        "wkv": flat(rows(f["L1_xattn_Wk"]), rows(f["L1_xattn_Wv"])),
        "l0x": flat(rows(w[:, :D].T), rows(w[:, D:].T)),
        "l0a": flat(rows(f["L0_attn_Wqkv"].T), rows(f["L0_attn_Wo"].T)),
        "l1a": flat(rows(qkv), rows(f["L1_attn_w_o"])),
        "l1x": flat(rows(f["L1_xattn_Wq"]), rows(f["L1_xattn_Wo"])),
        "bcol": flat(cols(b0[0]), cols(b0[1]), cols(f["L1_xattn_bq"]), cols(f["L1_xattn_bk"]), cols(bq[0]), cols(bq[1])),
        "brow": np.stack([f["L0_xattn_b"], b0[2], f["L0_attn_bo"], f["L1_xattn_bv"], f["L1_xattn_bo"], bq[2],
                          f["L1_attn_b_o"]]),
        "l0g": flat(rows(f["L0_ffn_gate_w"].T), rep(f["L0_ffn_gate_bias"])),
        "l0f": l0f,
        "l1g": flat(cols(f["L1_ffn_b1"]), rows(f["L1_ffn_gate_w"]), rep(f["L1_ffn_gate_b"])),
        "l1f": np.stack(l1f),
        "b2": np.ascontiguousarray(f["L1_ffn_b2"]),
        "lngb": np.stack([f["L1_ffn_ln_g"], f["L1_ffn_ln_b"]]),
    }


def kernel(**inputs):
    import concourse.bacc as _bacc
    from concourse.bass_utils import run_bass_kernel_spmd as _run

    arrays = layout(inputs)
    nc = _bacc.Bacc("TRN2", target_bir_lowering=False, num_devices=1)
    aps = {k: nc.dram_tensor(f"in_{k}", v.shape, mybir.dt.from_np(v.dtype), kind="ExternalInput").ap()
           for k, v in arrays.items()}
    aps["out"] = nc.dram_tensor("out_x", (P, 2, D), F32, kind="ExternalOutput").ap()
    build(nc, aps)
    r = _run(nc, [{f"in_{k}": v for k, v in arrays.items()}], core_ids=[0])
    y = r.results[0]["out_x"]
    return np.ascontiguousarray(np.asarray(y).transpose(1, 0, 2)).reshape(1, 256, D)
```

```python
from contextlib import ExitStack

import numpy as np

import concourse.bass as bass
from concourse import mybir

P = 128
F32 = mybir.dt.float32
F32R = mybir.dt.float32r
ALU = mybir.AluOpType
ACT = mybir.ActivationFunctionType
AX = mybir.AxisListType

D = 512
NC = 4
NCTX = 25088
GT = 256
NG = NCTX // GT
NT = NCTX // P
NCH = 4 * NT
H = 16
SCALE = float(1.0 / np.sqrt(np.float32(32.0)))
NEG = -1.0e30

C_L0Q, C_L0K, C_L1XQ, C_L1XK, C_L1AQ, C_L1AK = 0, 4, 8, 12, 16, 20
R_L0X, R_L0V, R_L0O, R_XV, R_XO, R_AV, R_AO = range(7)
BSLOT = [0, 1, 2, 3, 0, 1, 2]


CALLS = {
    "matmul": lambda e, a, k: e.matmul(*a, **k),
    "transpose": lambda e, a, k: e.transpose(*a, **k),
    "activation": lambda e, a, k: e.activation(*a, **k),
    "tensor_tensor": lambda e, a, k: e.tensor_tensor(*a, **k),
    "tensor_scalar": lambda e, a, k: e.tensor_scalar(*a, **k),
    "scalar_tensor_tensor": lambda e, a, k: e.scalar_tensor_tensor(*a, **k),
    "tensor_reduce": lambda e, a, k: e.tensor_reduce(*a, **k),
    "tensor_copy": lambda e, a, k: e.tensor_copy(*a, **k),
    "reciprocal": lambda e, a, k: e.reciprocal(*a, **k),
    "memset": lambda e, a, k: e.memset(*a, **k),
    "affine_select": lambda e, a, k: e.affine_select(*a, **k),
    "bn_stats": lambda e, a, k: e.bn_stats(*a, **k),
    "bn_aggr": lambda e, a, k: e.bn_aggr(*a, **k),
    "dma_start": lambda e, a, k: e.dma_start(*a, **k),
}


class Noted:


    def matmul(self, *a, **k):
        return "matmul", a, k

    def transpose(self, *a, **k):
        return "transpose", a, k

    def activation(self, *a, **k):
        return "activation", a, k

    def tensor_tensor(self, *a, **k):
        return "tensor_tensor", a, k

    def tensor_scalar(self, *a, **k):
        return "tensor_scalar", a, k

    def scalar_tensor_tensor(self, *a, **k):
        return "scalar_tensor_tensor", a, k

    def tensor_reduce(self, *a, **k):
        return "tensor_reduce", a, k

    def tensor_copy(self, *a, **k):
        return "tensor_copy", a, k

    def reciprocal(self, *a, **k):
        return "reciprocal", a, k

    def memset(self, *a, **k):
        return "memset", a, k

    def affine_select(self, *a, **k):
        return "affine_select", a, k

    def bn_stats(self, *a, **k):
        return "bn_stats", a, k

    def bn_aggr(self, *a, **k):
        return "bn_aggr", a, k

    def dma_start(self, *a, **k):
        return "dma_start", a, k


class Queues:

    def __init__(self):
        self.q = {e: [] for e in ("pe", "act", "dve", "pool", "sp")}
        self.n = {e: 0 for e in self.q}
        self.seen = {e: {} for e in self.q}
        self.chained = False

    def op(self, eng, fn, *waits, inc=True):
        waits = [w for w in waits if w is not None]
        if self.chained and eng in ("act", "dve", "pool") and self.n[eng]:
            waits.append((eng, self.n[eng]))
        need = []
        for s, v in waits:
            if self.seen[eng].get(s, 0) < v:
                self.seen[eng][s] = v
                need.append((s, v))
        if inc:
            self.n[eng] += 1
        self.q[eng].append((need, fn(Noted()), eng if inc else None, 1))
        return (eng, self.n[eng])

    def dma(self, fn, sem, *waits):
        need = []
        for s, v in [w for w in waits if w is not None]:
            if self.seen["sp"].get(s, 0) < v:
                self.seen["sp"][s] = v
                need.append((s, v))
        self.n[sem] = self.n.get(sem, 0) + 16
        self.q["sp"].append((need, fn(Noted()), sem, 16))
        return (sem, self.n[sem])

    def play(self, eng, e, sems):
        for need, (name, args, kw), sem, by in self.q[eng]:
            for s, v in need:
                e.wait_ge(sems[s], v)
            ins = CALLS[name](e, args, kw)
            if sem is not None:
                ins.then_inc(sems[sem], by)


def build(nc, a):
    K = Queues()
    op, dma = K.op, K.dma
    ctx = ExitStack()
    with ctx:
        def sb(name, shape, dt=F32, over=None):
            return (over or ctx).enter_context(nc.sbuf_tensor(name, shape, dt))

        X = sb("X", [P, 2, D])
        XT = sb("XT", [P, NC, 256])
        BI = sb("BI", [P, 4, D])
        BC = sb("BC", [P, 24])
        ident = sb("ident", [P, P])
        mask0 = sb("mask0", [P, 384])
        mask1 = sb("mask1", [P, 256])
        lt = sb("lt", [P, 256])
        st = sb("st", [P, 2, 6])
        mv = sb("mv", [P, 2, 2])
        rstd = sb("rstd", [P, 2])
        half = sb("half", [P, 2])
        small = sb("small", [P, 1024])
        PB = ctx.enter_context(nc.psum_tensor("PB", [P, 8, 512], F32))

        kv_life, life = ExitStack(), ExitStack()
        WKV = sb("WKV", [P, 4, NC, D], F32R, kv_life)
        WA = sb("WA", [P, 8192], over=life)
        W0 = sb("W0", [P, 4096], over=life)
        AR = sb("AR", [P, 10752], over=life)

        def bank(b, o=0, n=512):
            return PB[:, b, o:o + n]

        K.chained = True
        m_x = dma(lambda e: e.dma_start(X[:, :, :], a["x"]), "d_x")
        m_wkv = dma(lambda e: e.dma_start(WA[:, 0:4096], a["wkv"]), "d_wa")
        m_bc = dma(lambda e: e.dma_start(BC[:, :], a["bcol"]), "d_bc")

        def load_bias(r, *w):
            s = BSLOT[r]
            return dma(lambda e: e.dma_start(BI[:, s, :], a["brow"][r:r + 1, :].to_broadcast([P, D])),
                       f"d_bi{s}", *w)

        m_bi = {r: load_bias(r) for r in (R_L0X, R_L0V, R_L0O, R_XV)}
        m_l0x = dma(lambda e: e.dma_start(W0[:, :], a["l0x"]), "d_w0")

        op("pool", lambda e: e.memset(half[:, :], -0.5))
        op("pool", lambda e: e.memset(ident[:, :], 0.0))
        op("pool", lambda e: e.affine_select(out=ident[:, :], in_=ident[:, :], compare_op=ALU.not_equal,
                                             fill=1.0, base=0, pattern=[[-1, P]], channel_multiplier=1))
        op("pool", lambda e: e.memset(mask0[:, :], 0.0))
        op("pool", lambda e: e.affine_select(out=mask0[:, 0:128], in_=mask0[:, 0:128], compare_op=ALU.is_ge,
                                             fill=NEG, base=0, pattern=[[-1, P]], channel_multiplier=1))
        op("pool", lambda e: e.affine_select(out=mask0[:, 128:256], in_=mask0[:, 128:256], compare_op=ALU.is_ge,
                                             fill=NEG, base=-1, pattern=[[1, P]], channel_multiplier=-1))
        op("pool", lambda e: e.affine_select(out=mask0[:, 256:384], in_=mask0[:, 256:384], compare_op=ALU.is_ge,
                                             fill=NEG, base=0, pattern=[[-1, P]], channel_multiplier=1))
        op("pool", lambda e: e.memset(mask1[:, :], 0.0))
        for w in range(2):
            op("pool", lambda e, w=w: e.memset(mask1[0:64, 128 * w + 64:128 * w + 128], NEG))
            op("pool", lambda e, w=w: e.memset(mask1[64:128, 128 * w:128 * w + 64], NEG))
        op("pool", lambda e: e.memset(lt[:, :], 1.0))
        op("pool", lambda e: e.affine_select(out=lt[:, :].rearrange("p (a b) -> p a b", a=16),
                                             in_=lt[:, :].rearrange("p (a b) -> p a b", a=16),
                                             compare_op=ALU.is_gt, fill=0.0, base=0,
                                             pattern=[[1, 16], [-1, 16]], channel_multiplier=0))
        m_const = (op("pool", lambda e: e.memset(small[:, 1000:1024], 0.0)))
        wraw = WA[:, 0:4096].rearrange("p (m c n) -> p m c n", m=2, c=NC)
        for m in range(2):
            hi = op("act", lambda e, m=m: e.activation(WKV[:, 2 * m, :, :], wraw[:, m], ACT.Copy), m_wkv)
            m_wsplit = op("dve", lambda e, m=m: e.tensor_tensor(
                WKV[:, 2 * m + 1, :, :], wraw[:, m], WKV[:, 2 * m, :, :].bitcast(F32), ALU.subtract), m_wkv, hi)
        m_wl0 = dma(lambda e: e.dma_start(WA[:, :], a["l0a"]), "d_wa", m_wsplit)

        NP1 = NG // 2
        sums = small[:, 0:4 * NG]
        m_red = []
        for n in range(NP1):
            r = n % 4
            m = dma(lambda e, n=n, r=r: e.dma_start(
                AR[:, 2048 * r:2048 * r + 2048].rearrange("p (g f) -> p g f", g=2),
                a["ctx"][2 * n:2 * n + 2].rearrange("g p f -> p g f")), f"d_c{r}",
                m_red[n - 4] if n >= 4 else None)
            m_red.append(op("dve", lambda e, n=n, r=r: e.tensor_reduce(
                sums[:, 8 * n:8 * n + 8], AR[:, 2048 * r:2048 * r + 2048].rearrange("p (g f) -> p g f", f=GT),
                axis=AX.X, op=ALU.add), m))
        csum = small[:, 400:404]
        op("dve", lambda e: e.tensor_reduce(csum, sums.rearrange("p (g c) -> p c g", c=NC), axis=AX.X, op=ALU.add))
        SBC = AR[:, 0:512].rearrange("p (c i) -> p c i", c=NC)
        m_sbc = op("dve", lambda e: e.tensor_scalar(SBC, csum.unsqueeze(2).to_broadcast([P, NC, P]),
                                                    1.0 / NCTX, None, ALU.mult))

        def layernorm(XN, *w):
            for i in range(2):
                op("dve", lambda e, i=i: e.bn_stats(st[:, i, :], X[:, i, :]), *w)
                m = op("dve", lambda e, i=i: e.bn_aggr(mv[:, i, :], st[:, i, :]))
            op("pool", lambda e: e.tensor_scalar(rstd[:, :], mv[:, :, 1], 1e-5, None, ALU.add), m)
            m = op("pool", lambda e: e.tensor_tensor(rstd[:, :], rstd[:, :], half[:, :], ALU.pow))
            for i in range(2):
                m = op("dve", lambda e, i=i: e.tensor_scalar(
                    XN[:, i, :], X[:, i, :], mv[:, i, 0:1], rstd[:, i:i + 1], ALU.subtract, ALU.mult), m)
            return m

        def transpose_to(dst, src, m_src, *w, roll=0, unroll=0):
            for c in range(NC):
                for i in range(2):
                    m = op("pe", lambda e, c=c, i=i: e.transpose(
                        bank(c // 2, 256 * (c % 2) + 128 * i, 128), src[:, i, 128 * c:128 * c + 128], ident[:, :]),
                        m_src, m_const, *w, inc=(c % 2 == 1 and i == 1))
                if c % 2:
                    b = c // 2
                    d = dst[:, 2 * b:2 * b + 2, :]
                    s = bank(b).rearrange("p (c i) -> p c i", c=2)
                    if not roll:
                        out = op("act" if b else "dve", lambda e, d=d, s=s, b=b: (
                            e.activation(d, s, ACT.Copy) if b else e.tensor_copy(d, s)), m)
                    else:
                        op("dve", lambda e, d=d, s=s: e.tensor_copy(d[:, :, 0:256 - roll], s[:, :, roll:256]), m)
                        out = op("dve", lambda e, d=d, s=s: e.tensor_copy(d[:, :, 256 - roll:256], s[:, :, 0:roll]))
                    if not b:
                        first = out
            return [first, out]

        def last(eng):
            return (eng, K.n[eng])

        XN = AR[:, 9728:10752].rearrange("p (i n) -> p i n", i=2)
        m = layernorm(XN, m_x)
        m_xt = transpose_to(XT, XN, m)
        for i in range(2):
            m_xb = op("dve", lambda e, i=i: e.tensor_tensor(X[:, i, :], X[:, i, :], BI[:, 0, :], ALU.add), m_bi[R_L0X])
        w0 = W0[:, :].rearrange("p (m c n) -> p m c n", m=2, c=NC)
        for i in range(2):
            for c in range(NC):
                op("pe", lambda e, i=i, c=c: e.matmul(bank(2 + i), XT[:, c, 128 * i:128 * i + 128], w0[:, 0, c, :],
                                                      start=(c == 0), stop=False), *m_xt, m_l0x, inc=False)
            for c in range(NC):
                m = op("pe", lambda e, i=i, c=c: e.matmul(bank(2 + i), SBC[:, c, :], w0[:, 1, c, :],
                                                          start=False, stop=(c == NC - 1)), m_sbc, inc=(c == NC - 1))
            m_xr = op("dve", lambda e, i=i: e.tensor_tensor(X[:, i, :], X[:, i, :], bank(2 + i), ALU.add), m)
        m_bi[R_XO] = load_bias(R_XO, m_xb)

        def self_attention(WA, AR, cq, ck, rv, ro, m_w, mask, blocks, roll):
            NB = len(blocks)
            W = 128 * NB
            XN = AR[:, 9728:9728 + 1024].rearrange("p (i n) -> p i n", i=2)
            QT = AR[:, 0:0 + 1024].rearrange("p (c i) -> p c i", c=NC)
            KT = AR[:, 1024:1024 + 1024].rearrange("p (c i) -> p c i", c=NC)
            V = AR[:, 2048:2048 + 1024].rearrange("p (i n) -> p i n", i=2)
            SM = AR[:, 3072:3072 + 2 * 4 * W].rearrange("p (b s w) -> p b s w", b=2, s=4)
            PT = AR[:, 6144:6144 + 4 * W].rearrange("p (s w) -> p s w", s=4)
            AT = AR[:, 7680:7680 + 1024].rearrange("p (i n) -> p i n", i=2)
            ATT = AR[:, 8704:8704 + 1024].rearrange("p (c i) -> p c i", c=NC)
            wq = WA[:, 0:6144].rearrange("p (c n) -> p c n", c=NC)
            wo = WA[:, 6144:8192].rearrange("p (c n) -> p c n", c=NC)
            nm = small[:, 0:8].rearrange("p (s i) -> p s i", i=2)
            su = small[:, 16:48].rearrange("p (h i) -> p h i", i=2)
            rc = small[:, 48:80].rearrange("p (h i) -> p h i", i=2)
            m = layernorm(XN, last("pe"))
            m_xt = transpose_to(XT, XN, m, roll=roll)
            for m8 in range(8):
                b = 2 + m8 // 2
                o = 256 * (m8 % 2)
                for c in range(NC):
                    m = op("pe", lambda e, m8=m8, c=c, b=b, o=o: e.matmul(
                        bank(b, o, 256), wq[:, c, 128 * m8:128 * m8 + 128], XT[:, c, :],
                        start=(c == 0), stop=(c == NC - 1)), *m_xt, m_w, inc=(c == NC - 1))
                if m8 % 2:
                    for z in (m8 - 1, m8):
                        oz = 256 * (z % 2)
                        if z < 4:
                            m_q = op("dve", lambda e, z=z, b=b, oz=oz: e.tensor_scalar(
                                QT[:, z, :], bank(b, oz, 256), BC[:, cq + z:cq + z + 1], SCALE, ALU.add, ALU.mult),
                                m, m_bc)
                        else:
                            m_q = op("dve", lambda e, z=z, b=b, oz=oz: e.tensor_scalar(
                                KT[:, z - 4, :], bank(b, oz, 256), BC[:, ck + z - 4:ck + z - 3], None, ALU.add),
                                m, m_bc)
            for i in range(2):
                for c in range(NC):
                    m = op("pe", lambda e, i=i, c=c: e.matmul(
                        bank(6 + i), XT[:, c, 128 * i:128 * i + 128], wq[:, c, 1024:1536],
                        start=(c == 0), stop=(c == NC - 1)), inc=(c == NC - 1))
                m_v = op("dve", lambda e, i=i: e.tensor_tensor(V[:, i, :], bank(6 + i), BI[:, BSLOT[rv], :], ALU.add),
                         m, m_bi[rv])
            for i in range(2):
                m_xb = op("dve", lambda e, i=i: e.tensor_tensor(X[:, i, :], X[:, i, :], BI[:, BSLOT[ro], :], ALU.add),
                          m_bi[ro])
            m_sm, m_tr, m_pt = {}, {}, {}
            rng = {i: [z for z, (q, _) in enumerate(blocks) if q == i] for i in range(2)}
            m_ex = {}

            def scores(c):
                for s in range(4):
                    for i in range(2):
                        z0, nz = rng[i][0], len(rng[i])
                        j0 = blocks[z0][1]
                        m = op("pe", lambda e, s=s, i=i, z0=z0, nz=nz, j0=j0: e.matmul(
                            bank(s, 128 * z0, 128 * nz), QT[32 * s:32 * s + 32, c, 128 * i:128 * i + 128],
                            KT[32 * s:32 * s + 32, c, 128 * j0:128 * (j0 + nz)], start=True, stop=True),
                            m_q, m_sm.get(c - 1), inc=(s == 3 and i == 1))
                b = c % 2
                m_sm[c] = op("dve", lambda e: e.tensor_tensor(
                    SM[:, b], PB[:, 0:4, 0:W], mask[:, 0:W].unsqueeze(1).to_broadcast([P, 4, W]), ALU.add),
                    m, m_tr.get(c - 2))
                for i in range(2):
                    z0, nz = rng[i][0], len(rng[i])
                    m = op("dve", lambda e, i=i, z0=z0, nz=nz: e.tensor_reduce(
                        nm[:, :, i], SM[:, b, :, 128 * z0:128 * (z0 + nz)], axis=AX.X, op=ALU.max, negate=True),
                        m_ex.get(c - 1))
                for s in range(4):
                    for i in range(2):
                        z0, nz = rng[i][0], len(rng[i])
                        v = SM[:, b, s, 128 * z0:128 * (z0 + nz)]
                        m_ex[c] = op("act", lambda e, s=s, i=i, v=v: e.activation(
                            v, v, ACT.Exp, bias=nm[:, s, i:i + 1], accum_out=su[:, 4 * c + s, i:i + 1]), m)

            def mix(c):
                for s in range(4):
                    pb = 4 + s % 2
                    for z in range(NB):
                        m = op("pe", lambda e, s=s, z=z, pb=pb: e.transpose(
                            bank(pb, 128 * z, 128), SM[:, c % 2, s, 128 * z:128 * z + 128], ident[:, :]),
                            m_ex[c], m_pt.get(4 * c + s - 2), inc=(z == NB - 1))
                    m_tr[c] = m
                    m_pt[4 * c + s] = op("dve", lambda e, s=s, pb=pb: e.tensor_copy(
                        PT[:, s, :], bank(pb, 0, W)), m, m_pvs.get(4 * c + s - 4))
                    h = 4 * c + s
                    for z, (i, j) in enumerate(blocks):
                        m_pvs[h] = op("pe", lambda e, s=s, h=h, z=z, i=i, j=j: e.matmul(
                            bank(6 + i, 32 * h, 32), PT[:, s, 128 * z:128 * z + 128], V[:, j, 32 * h:32 * h + 32],
                            start=(z == rng[i][0]), stop=(z == rng[i][-1])), m_pt[4 * c + s], m_v, inc=(z == NB - 1))

            m_pvs = {}
            scores(0)
            for c in range(NC):
                if c + 1 < NC:
                    scores(c + 1)
                mix(c)
            m = op("dve", lambda e: e.reciprocal(rc, su), m_ex[3])
            for i in range(2):
                m = op("dve", lambda e, i=i: e.tensor_tensor(
                    AT[:, i, :].rearrange("p (h d) -> p h d", h=H), bank(6 + i).rearrange("p (h d) -> p h d", h=H),
                    rc[:, :, i].unsqueeze(2).to_broadcast([P, H, 32]), ALU.mult), m_pvs[15])
            m_at = transpose_to(ATT, AT, m, m_sm[3], roll=(256 - roll) % 256)
            for i in range(2):
                for c in range(NC):
                    m = op("pe", lambda e, i=i, c=c: e.matmul(
                        bank(2 + i), ATT[:, c, 128 * i:128 * i + 128], wo[:, c, :],
                        start=(c == 0), stop=(c == NC - 1)), *m_at, inc=(c == NC - 1))
                op("dve", lambda e, i=i: e.tensor_tensor(X[:, i, :], X[:, i, :], bank(2 + i), ALU.add), m)
            return m_xb

        m_xb = self_attention(WA, AR, C_L0Q, C_L0K, R_L0V, R_L0O, m_wl0, mask0, [(0, 0), (1, 0), (1, 1)], 0)
        m_bi[R_AV] = load_bias(R_AV, m_xb)
        m_bi[R_AO] = load_bias(R_AO, m_xb)
        life.close()

        def ranks(dst, v, E, tmp, n=1):
            g = tmp.rearrange("p (g a b) -> p g a b", g=n, a=E)
            t = small[:, 512:512 + n * E * E].rearrange("p (g a b) -> p g a b", g=n, a=E)
            for x in range(n):
                vv = v[:, x * E:(x + 1) * E]
                o = vv.unsqueeze(1).to_broadcast([P, E, E])
                s = vv.unsqueeze(2).to_broadcast([P, E, E])
                l = lt[:, :].rearrange("p (a b) -> p a b", a=16)[:, 0:E, 0:E]
                op("dve", lambda e, x=x, o=o, s=s: e.tensor_tensor(g[:, x], o, s, ALU.is_equal))
                op("dve", lambda e, x=x, l=l: e.tensor_tensor(g[:, x], g[:, x], l, ALU.mult), m_const)
                op("dve", lambda e, x=x, o=o, s=s: e.tensor_tensor(t[:, x], o, s, ALU.is_gt))
                op("dve", lambda e, x=x: e.tensor_tensor(g[:, x], g[:, x], t[:, x], ALU.add))
                op("dve", lambda e, x=x: e.tensor_reduce(dst[:, x * E:(x + 1) * E], g[:, x], axis=AX.X, op=ALU.add))

        life = ExitStack()
        WF = sb("WF", [P, 2, 3, 1536], over=life)
        WS = sb("WS", [P, 2, 3, 2, 1536], F32R, life)
        XS = sb("XS", [P, 2, NC, 256], F32R, life)
        HS = sb("HS", [P, 2, 3, 2, 256], F32R, life)
        HF = sb("HF", [P, 2, 3, 256], over=life)
        XNF = WF[:, 1, 0:2, :].rearrange("p m n -> p (m n)")[:, 0:1024].rearrange("p (i n) -> p i n", i=2)
        gw = small[:, 0:64].rearrange("p (c n) -> p c n", c=NC)
        m = layernorm(XNF, last("pe"))
        gb = small[:, 64:80]
        m_gw = dma(lambda e: e.dma_start(small[:, 0:80], a["l0g"]), "d_g", last("dve"), last("act"))
        m_xt = transpose_to(XT, XNF, m)
        comb = small[:, 80:112].rearrange("p (i n) -> p i n", i=2)
        sc, v, rk, t16 = small[:, 112:128], small[:, 128:144], small[:, 144:160], small[:, 160:176]
        gs, gm, t1 = small[:, 176:180], small[:, 180:184], small[:, 184:185]
        tmp = small[:, 768:1024]
        for i in range(2):
            for c in range(NC):
                m = op("pe", lambda e, i=i, c=c: e.matmul(bank(3, 16 * i, 16), XT[:, c, 128 * i:128 * i + 128],
                                                          gw[:, c, :], start=(c == 0), stop=(c == NC - 1)),
                       *m_xt, m_gw, inc=(c == NC - 1))
        m_gate = m
        for i in range(2):
            m = op("act", lambda e, i=i: e.activation(sc, bank(3, 16 * i, 16), ACT.Sigmoid), m_gate, last("dve"))
            op("dve", lambda e: e.tensor_tensor(v, sc, gb, ALU.add), m)
            ranks(rk, v, 4, tmp[:, 0:64], n=4)
            op("dve", lambda e: e.tensor_scalar(t16, rk, 2.0, None, ALU.is_lt))
            op("dve", lambda e: e.tensor_tensor(t16, t16, v, ALU.mult))
            op("dve", lambda e: e.tensor_reduce(gs, t16.rearrange("p (g a) -> p g a", g=4), axis=AX.X, op=ALU.add))
            ranks(gm, gs, 4, tmp[:, 0:16])
            op("dve", lambda e: e.tensor_scalar(gm, gm, 2.0, None, ALU.is_lt))
            gmb = gm.unsqueeze(2).to_broadcast([P, 4, 4])
            v4 = v.rearrange("p (g a) -> p g a", g=4)
            t4 = t16.rearrange("p (g a) -> p g a", g=4)
            op("dve", lambda e: e.tensor_tensor(v4, v4, gmb, ALU.mult))
            op("dve", lambda e: e.tensor_scalar(t4, gmb, -1.0, 1.0e30, ALU.add, ALU.mult))
            op("dve", lambda e: e.tensor_tensor(v, v, t16, ALU.add))
            ranks(rk, v, 16, tmp)
            op("dve", lambda e: e.tensor_scalar(t16, rk, 4.0, None, ALU.is_lt))
            op("dve", lambda e: e.tensor_tensor(t16, t16, sc, ALU.mult))
            op("dve", lambda e: e.tensor_reduce(t1, t16, axis=AX.X, op=ALU.add))
            op("dve", lambda e: e.tensor_scalar(t1, t1, 1e-20, None, ALU.add))
            op("dve", lambda e: e.reciprocal(t1, t1))
            op("dve", lambda e, i=i: e.tensor_scalar(comb[:, i, :], t16, t1, 2.5, ALU.mult, ALU.mult))
        split_xt = lambda XS: (
            op("dve", lambda e: e.tensor_copy(XS[:, 0], XT[:, :, :]), *m_xt),
            op("dve", lambda e: e.tensor_tensor(XS[:, 1], XT[:, :, :], XS[:, 0].bitcast(F32), ALU.subtract)))[1]
        m_xs = split_xt(XS)
        m_start = [last("pe"), last("dve"), last("act")]
        K.chained = False
        m_hf, m_free, m_acc, m_h, m_w, m_sp, m_dn, m_up = ({} for _ in range(8))

        def load0(x):
            m_w[x] = dma(lambda e: e.dma_start(WF[:, x % 2].rearrange("p m f -> p (m f)"), a["l0f"][x]),
                         f"d_f{x % 2}", m_sp.get((x - 2, 2)), *m_start)

        def split0(x, m):
            r = x % 2
            hi = op("act", lambda e: e.activation(WS[:, r, m, 0, :], WF[:, r, m, :], ACT.Copy), m_w[x],
                    (m_up if m < 2 else m_dn).get(x - 2), *m_start)
            m_sp[x, m] = op("dve", lambda e: e.tensor_tensor(
                WS[:, r, m, 1, :], WF[:, r, m, :], WS[:, r, m, 0, :].bitcast(F32), ALU.subtract), hi)
            if m == 2 and x + 2 < 17:
                load0(x + 2)

        def up0(x, k):
            r, n = x % 2, 3 * x + k
            for u in range(2):
                q = 0
                for wh, xh in ((0, 0), (0, 1), (1, 0)):
                    w = WS[:, r, u, wh, :].rearrange("p (c n) -> p c n", c=NC)
                    for c in range(NC):
                        q += 1
                        m = op("pe", lambda e, w=w, c=c, xh=xh, q=q, u=u: e.matmul(
                            bank(k, 256 * u, 256), w[:, c, 128 * k:128 * k + 128], XS[:, xh, c, :],
                            start=(q == 1), stop=(q == 12)), m_sp[x, u], m_hf.get(n - 3), m_xs, inc=(u == 1 and q == 12))
            m_up[x] = m
            ms = op("act", lambda e: e.activation(HF[:, 0, k, :], bank(k, 0, 256), ACT.Silu), m, m_hf.get(n - 3),
                    *m_start)
            m_hf[n] = op("dve", lambda e: e.tensor_tensor(
                HF[:, 1, k, :], HF[:, 0, k, :], bank(k, 256, 256), ALU.mult), ms, m_h.get(n - 3))
            hi = op("dve", lambda e: e.tensor_copy(HS[:, r, k, 0, :], HF[:, 1, k, :]), m_hf[n], m_dn.get(x - 2))
            m_h[n] = op("pool", lambda e: e.tensor_tensor(
                HS[:, r, k, 1, :], HF[:, 1, k, :], HS[:, r, k, 0, :].bitcast(F32), ALU.subtract), hi)

        def down0(x, i):
            r = x % 2
            b = 4 + 2 * r + i
            steps = [(hh, wh, k) for k in range(3) for hh, wh in ((0, 0), (0, 1), (1, 0))]
            for q, (hh, wh, k) in enumerate(steps):
                w = WS[:, r, 2, wh, :].rearrange("p (k n) -> p k n", k=3)
                m = op("pe", lambda e, hh=hh, w=w, k=k, q=q: e.matmul(
                    bank(b), HS[:, r, k, hh, 128 * i:128 * i + 128], w[:, k, :], start=(q == 0), stop=(q == 8)),
                    m_h[3 * x + k], m_sp[x, 2], m_acc.get((x - 2, i)), inc=(q == 8))
            s = comb[:, i, x:x + 1] if x < 16 else 1.0
            m_acc[x, i] = op("dve", lambda e: e.scalar_tensor_tensor(
                out=X[:, i, :], in0=bank(b), scalar=s, in1=X[:, i, :], op0=ALU.mult, op1=ALU.add),
                m, m_acc.get((x - 1, i)), *m_start)
            m_dn[x] = m

        load0(0)
        load0(1)
        for m in range(3):
            split0(0, m)
        for x in range(17):
            for k in range(3):
                up0(x, k)
                if x and k:
                    down0(x - 1, k - 1)
                if x + 1 < 17:
                    split0(x + 1, k)
        down0(16, 0)
        down0(16, 1)
        K.chained = True
        life.close()

        life = ExitStack()
        CTX = sb("CTX", [P, 3, 2, NC, GT], F32R, life)
        KHL = sb("KHL", [P, 2, 2, NC, GT], F32R, life)
        STK = sb("STK", [P, 2, 4, NC, GT], F32R, life)
        QS = sb("QS", [P, 4, NC, 256], F32R, life)
        RAW = sb("RAW", [P, 3, NC * GT], over=life)
        V = sb("V", [P, 2, D], over=life)
        VS = sb("VS", [P, 4, P], over=life)
        EE = sb("EE", [P, 4, 4, 256], over=life)
        OT = sb("OT", [P, NC, 256], over=life)
        WO = sb("WO", [P, NC, D], over=life)
        raw = lambda r: RAW[:, r, :]
        wq = EE[:, 0:2].rearrange("p b s i -> p (b s i)").rearrange("p (c n) -> p c n", c=NC)
        XNX = EE[:, 2].rearrange("p s i -> p (s i)").rearrange("p (i n) -> p i n", i=2)
        qf = EE[:, 3].rearrange("p c i -> p (c i)")
        QHL = KHL
        wo = WO
        m_end = [last("pe"), last("dve"), last("act"), last("pool")]
        m_wx = dma(lambda e: e.dma_start(wq, a["l1x"][:, 0:2048].rearrange("p (c n) -> p c n", c=NC)), "d_w0", *m_end)
        m_wo = dma(lambda e: e.dma_start(WO[:, :, :], a["l1x"][:, 2048:4096].rearrange("p (c n) -> p c n", c=NC)),
                   "d_x", *m_end)
        m_raw, m_lo = {}, {}

        def load_ctx(g):
            m_raw[g] = dma(lambda e: e.dma_start(raw(g % 3), a["ctx"][g]), f"d_c{g % 3}", m_lo.get(g - 3), *m_end)

        for g in range(3):
            load_ctx(g)
        m = layernorm(XNX, *m_end)
        m_xt = transpose_to(XT, XNX, m)
        for c4 in range(NC):
            for c in range(NC):
                m = op("pe", lambda e, c=c, c4=c4: e.matmul(
                    bank(2 + c4, 0, 256), wq[:, c, 128 * c4:128 * c4 + 128], XT[:, c, :],
                    start=(c == 0), stop=(c == NC - 1)), *m_xt, m_wx, inc=(c == NC - 1))
            m = op("dve", lambda e, c4=c4: e.tensor_scalar(
                qf[:, 256 * c4:256 * c4 + 256], bank(2 + c4, 0, 256), BC[:, C_L1XQ + c4:C_L1XQ + c4 + 1], SCALE,
                ALU.add, ALU.mult), m)
        hl = [KHL[:, 0, h].rearrange("p c j -> p (c j)") for h in range(2)]
        op("dve", lambda e: e.tensor_copy(hl[0], qf))
        m = op("dve", lambda e: e.tensor_tensor(hl[1], qf, hl[0].bitcast(F32), ALU.subtract))

        def stack(dst, src, kinds, sem, *w):
            for s in range(4):
                for q in range(4):
                    m = dma(lambda e, s=s, q=q: e.dma_start(
                        dst[32 * q:32 * q + 32, s, :, :].bitcast(F32),
                        src[32 * s:32 * s + 32, kinds[q], :, :].bitcast(F32)), sem, *w)
            return m

        m_q = stack(QS, KHL[:, 0], (0, 0, 1, 1), "d_q", m)
        for i in range(2):
            op("dve", lambda e, i=i: e.tensor_tensor(X[:, i, :], X[:, i, :], BI[:, BSLOT[R_XO], :], ALU.add),
               m_bi[R_XO])
        m_pro = last("dve")
        K.chained = False

        nm = small[:, 0:16].rearrange("p (b s) -> p b s", b=4)
        su = small[:, 16:32].rearrange("p (b s) -> p b s", b=4)
        rc = small[:, 32:48].rearrange("p (b s) -> p b s", b=4)
        m_khi, m_klo, m_kp, m_vp, m_vev, m_vs, m_ex, m_mx, m_rc, m_pv, m_s = ({} for _ in range(11))

        def split_ctx(g):
            b = g % 3
            hi = op("dve", lambda e: e.tensor_copy(CTX[:, b, 0, :, :].rearrange("p c j -> p (c j)"), raw(g % 3)),
                    m_raw[g], m_vp.get(2 * (g - 3) + 1), m_kp.get((g - 3, 3)))
            m_lo[g] = op("pool", lambda e: e.tensor_tensor(
                CTX[:, b, 1, :, :].rearrange("p c j -> p (c j)"), raw(g % 3),
                CTX[:, b, 0, :, :].rearrange("p c j -> p (c j)").bitcast(F32), ALU.subtract), hi)
            if g + 3 < NG:
                load_ctx(g + 3)

        def project_k(g, ch):
            b = g % 3
            n = 0
            for wh, xh in ((0, 0), (0, 1), (1, 0)):
                for c in range(NC):
                    n += 1
                    m = op("pe", lambda e, wh=wh, xh=xh, c=c, n=n: e.matmul(
                        bank(4, 0, GT), WKV[:, wh, c, 128 * ch:128 * ch + 128], CTX[:, b, xh, c, :],
                        start=(n == 1), stop=(n == 12)), m_lo[g], m_klo.get(m_kprev[0]), inc=(n == 12))
            m_kp[g, ch] = m
            m_kprev[0] = (g, ch)

        m_kprev = [None]
        m_stk = {}

        def stack_k(g):
            m_stk[g] = stack(STK[:, g % 2], KHL[:, g % 2], (0, 1, 0, 1), f"d_s{g % 2}", m_klo[g, 3],
                             m_s.get(8 * (g - 2) + 7))


        def evac_k_hi(g, ch):
            m_khi[g, ch] = op("act", lambda e: e.activation(
                KHL[:, g % 2, 0, ch, :], bank(4, 0, GT), ACT.Identity, bias=BC[:, C_L1XK + ch:C_L1XK + ch + 1]),
                m_kp[g, ch], m_stk.get(g - 2), m_q)

        def evac_k_lo(g, ch):
            m_klo[g, ch] = op("dve", lambda e: e.scalar_tensor_tensor(
                out=KHL[:, g % 2, 1, ch, :], in0=bank(4, 0, GT), scalar=BC[:, C_L1XK + ch:C_L1XK + ch + 1],
                in1=KHL[:, g % 2, 0, ch, :].bitcast(F32), op0=ALU.add, op1=ALU.subtract), m_khi[g, ch])

        def project_v(t, half):
            g, b, j = t // 2, (t // 2) % 3, 128 * (t % 2)
            steps = [(xh, wh, c) for xh, wh in ((0, 0), (0, 1), (1, 0)) for c in range(NC)]
            for n in range(6 * half, 6 * half + 6):
                xh, wh, c = steps[n]
                m = op("pe", lambda e, xh=xh, wh=wh, c=c, n=n: e.matmul(
                    bank(5), CTX[:, b, xh, c, j:j + 128], WKV[:, 2 + wh, c, :],
                    start=(n == 0), stop=(n == 11)), m_lo[g], m_vev.get(t - 1), inc=(n == 11))
            if half:
                m_vp[t] = m

        def evac_v(t):
            m_vev[t] = op("dve", lambda e: e.tensor_tensor(V[:, t % 2, :], bank(5), BI[:, BSLOT[R_XV], :], ALU.add),
                          m_vp[t], m_vs.get(4 * (t - 2) + 3), m_bi[R_XV])

        def scores(k):
            t, c = k // 4, k % 4
            g, b, j = t // 2, (t // 2) % 2, 128 * (t % 2)
            for s in range(4):
                o = bank(2 * (k % 2) + s // 2, 256 * (s % 2), 256)
                m = op("pe", lambda e, o=o, s=s: e.matmul(
                    o, STK[:, b, s, c, j:j + 128], QS[:, s, c, :], start=True, stop=True),
                    m_stk[g], m_ex.get(k - 2), m_pro, m_q, inc=(s == 3))
            m_s[k] = m

        def softmax(k):
            b = k % 4
            pb = 2 * (k % 2)
            m_mx[k] = op("dve", lambda e: e.tensor_reduce(
                nm[:, b, :].rearrange("p (a s) -> p a s", a=2),
                PB[:, pb:pb + 2, :].rearrange("p a (s i) -> p a s i", s=2), axis=AX.X, op=ALU.max, negate=True),
                m_s[k], m_ex.get(k - 4))
            for s in range(4):
                m = op("act", lambda e, s=s: e.activation(
                    EE[:, b, s, :], bank(pb + s // 2, 256 * (s % 2), 256), ACT.Exp, bias=nm[:, b, s:s + 1],
                    accum_out=su[:, b, s:s + 1]), m_mx[k], m_pv.get(k - 4), m_rc.get(k - 4), inc=(s == 3))
            m_ex[k] = m

        def scale_v(k):
            b, t, c = k % 4, k // 4, k % 4
            m_rc[k] = op("dve", lambda e: e.reciprocal(rc[:, b, :], su[:, b, :]), m_ex[k], m_vs.get(k - 4))
            m_vs[k] = op("pool", lambda e: e.tensor_tensor(
                VS[:, b, :].rearrange("p (s d) -> p s d", s=4),
                V[:, t % 2, 128 * c:128 * c + 128].rearrange("p (s d) -> p s d", s=4),
                rc[:, b, :].unsqueeze(2).to_broadcast([P, 4, 32]), ALU.mult), m_rc[k], m_pv.get(k - 4), m_vev[t])

        def mix(k):
            t, c, b = k // 4, k % 4, k % 4
            for s in range(4):
                m = op("pe", lambda e, s=s: e.matmul(
                    PB[32 * s:32 * s + 32, 6 + c // 2, 256 * (c % 2):256 * (c % 2) + 256],
                    VS[:, b, 32 * s:32 * s + 32], EE[:, b, s, :],
                    start=(t == 0 and c % 2 == 0), stop=(t == NT - 1), skip_group_check=True),
                    m_vs[k], m_ex[k], inc=(s == 3))
            m_pv[k] = m

        for g in range(2):
            split_ctx(g)
            for ch in range(4):
                project_k(g, ch)
                evac_k_hi(g, ch)
                evac_k_lo(g, ch)
            stack_k(g)
        project_v(0, 0)
        project_v(0, 1)
        evac_v(0)
        split_ctx(2)
        lo_due = []
        for k in range(NCH):
            t, c = k // 4, k % 4
            g, tt = t // 2, t % 2
            scores(k)
            softmax(k)
            if k >= 1:
                scale_v(k - 1)
            for due in lo_due:
                evac_k_lo(*due)
            if k % 8 == 7 and g + 2 < NG:
                stack_k(g + 2)
            lo_due = []
            if c % 2 == 0:
                if g + 2 < NG:
                    ch = 2 * tt + c // 2
                    project_k(g + 2, ch)
                    evac_k_hi(g + 2, ch)
                    lo_due.append((g + 2, ch))
            elif t + 1 < NT:
                project_v(t + 1, c // 2)
                if c == 3:
                    evac_v(t + 1)
                    if tt == 0 and g + 3 < NG:
                        split_ctx(g + 3)
            if k >= 2:
                mix(k - 2)
        scale_v(NCH - 1)
        mix(NCH - 2)
        mix(NCH - 1)
        K.chained = True
        m = m_pv[NCH - 1]
        for b in range(2):
            m2 = op("act" if b else "dve", lambda e, b=b: (
                e.activation(OT[:, 2 * b:2 * b + 2, :].rearrange("p c i -> p (c i)"), bank(6 + b), ACT.Copy) if b
                else e.tensor_copy(OT[:, 0:2, :].rearrange("p c i -> p (c i)"), bank(6))), m)
        m1 = last("dve")
        for i in range(2):
            for c in range(NC):
                m = op("pe", lambda e, i=i, c=c: e.matmul(
                    bank(2 + i), OT[:, c, 128 * i:128 * i + 128], wo[:, c, :],
                    start=(c == 0), stop=(c == NC - 1)), m1, m2, m_wo, m_ex[NCH - 1], inc=(c == NC - 1))
            op("dve", lambda e, i=i: e.tensor_tensor(X[:, i, :], X[:, i, :], bank(2 + i), ALU.add), m)

        life.close()
        kv_life.close()
        life = ExitStack()
        RW = sb("RW", [P, 3, 4096], over=ctx)
        WL = sb("WL", [P, 8192], over=life)
        AL = sb("AL", [P, 10752], over=life)
        m_wl1 = dma(lambda e: e.dma_start(WL[:, :], a["l1a"]), "d_wa", last("pe"), last("dve"), last("act"),
                    last("pool"))
        m_wf, m_done, m_sp = {}, {}, {}
        NPC = 32

        def load_piece(n, *w):
            m_wf[n] = dma(lambda e: e.dma_start(RW[:, n % 3, :], a["l1f"][n]), f"d_f{n % 3}",
                          m_sp.get((n - 3, 1)), *w)

        for n in range(3):
            load_piece(n, m_wl1)
        self_attention(WL, AL, C_L1AQ, C_L1AK, R_AV, R_AO, m_wl1, mask1, [(0, 0), (1, 1)], 64)

        m_end = [last("pe"), last("dve"), last("act")]
        life.close()
        life = ctx
        WS1 = sb("WS1", [P, 2, 2, 2, 2048], F32R, life)
        XS1 = sb("XS1", [P, 2, NC, 256], F32R, life)
        HS1 = sb("HS1", [P, 4, 2, 256], F32R, life)
        HF1 = sb("HF1", [P, 4, 256], over=life)
        LN = sb("LN", [P, 2, D], over=life)
        MS = sb("MS", [P, 1024], over=life)
        ACC = sb("ACC", [P, 2, D], over=life)
        XNM = sb("XNM", [P, 2, D], over=life)
        lng, lnb = LN[:, 0], LN[:, 1]
        b2 = MS[0:8, 0:512]
        b1 = MS[:, 512:640]
        gw = MS[:, 640:672].rearrange("p (c n) -> p c n", c=NC)
        gbb = MS[:, 672:680]
        pT = MS[0:8, 768:1024].rearrange("p (i n) -> p i n", i=2)
        m_ln = dma(lambda e: e.dma_start(LN[:, :, :], a["lngb"].unsqueeze(0).to_broadcast([P, 2, D])), "d_w0", *m_end)
        m_b2 = dma(lambda e: e.dma_start(b2, a["b2"]), "d_x", *m_end)
        m_b1 = dma(lambda e: e.dma_start(MS[:, 512:680], a["l1g"]), "d_g", *m_end)
        m = layernorm(XNM, *m_end)
        m_xt = transpose_to(XT, XNM, m)
        for i in range(2):
            for c in range(NC):
                m = op("pe", lambda e, i=i, c=c: e.matmul(bank(3, 8 * i, 8), XT[:, c, 128 * i:128 * i + 128],
                                                          gw[:, c, :], start=(c == 0), stop=(c == NC - 1)),
                       *m_xt, m_b1, inc=(c == NC - 1))
        comb = small[:, 80:96].rearrange("p (i n) -> p i n", i=2)
        lg, rk, t8, mxv, sv = small[:, 112:120], small[:, 120:128], small[:, 128:136], small[:, 136:137], small[:, 137:138]
        m_gate = m
        for i in range(2):
            op("dve", lambda e, i=i: e.tensor_tensor(lg, bank(3, 8 * i, 8), gbb, ALU.add), m_gate, last("act"))
            op("dve", lambda e: e.tensor_scalar(lg, lg, 1.0 / 0.9, None, ALU.mult))
            ranks(rk, lg, 8, tmp[:, 0:64])
            m = op("dve", lambda e: e.tensor_reduce(mxv, lg, axis=AX.X, op=ALU.max, negate=True))
            m = op("act", lambda e: e.activation(t8, lg, ACT.Exp, bias=mxv), m)
            op("dve", lambda e: e.tensor_scalar(rk, rk, 2.0, None, ALU.is_lt))
            op("dve", lambda e: e.tensor_tensor(t8, t8, rk, ALU.mult), m)
            op("dve", lambda e: e.tensor_reduce(sv, t8, axis=AX.X, op=ALU.add))
            op("dve", lambda e: e.reciprocal(sv, sv))
            m_cb = op("dve", lambda e, i=i: e.tensor_scalar(comb[:, i, :], t8, sv, None, ALU.mult))
        for i in range(2):
            m = op("pe", lambda e, i=i: e.transpose(PB[0:8, 2, 128 * i:128 * i + 128], comb[:, i, :], ident[:, :]), m_cb)
        m = op("dve", lambda e: e.tensor_copy(pT, PB[0:8, 2, 0:256].rearrange("p (i n) -> p i n", i=2)), m)
        for i in range(2):
            m2 = op("pe", lambda e, i=i: e.matmul(bank(4 + i), pT[:, i, :], b2, start=True, stop=True), m, m_b2)
            op("dve", lambda e, i=i: e.tensor_copy(ACC[:, i, :], bank(4 + i)), m2, *m_end)
        m_xs = split_xt(XS1)
        m_start = [last("dve"), last("act"), last("pe")]
        K.chained = False
        m_g, m_h, m_dn, m_up, m_acc = {}, {}, {}, {}, {}

        def split1(n, w):
            src = RW[:, n % 3, 2048 * w:2048 * w + 2048]
            for p in range(2):
                z = slice(1024 * p, 1024 * p + 1024)
                hi = op("act", lambda e, z=z: e.activation(WS1[:, n % 2, w, 0, z], src[:, z], ACT.Copy), m_wf[n],
                        (m_dn if w else m_up).get(4 * (n - 2) + 3), *m_start)
                m_sp[n, w] = op("dve", lambda e, z=z: e.tensor_tensor(
                    WS1[:, n % 2, w, 1, z], src[:, z], WS1[:, n % 2, w, 0, z].bitcast(F32), ALU.subtract), hi)
            if w and n + 3 < NPC:
                load_piece(n + 3)

        def up1(n):
            pc, f = n // 4, n % 4
            q = 0
            for wh, xh in ((0, 0), (0, 1), (1, 0)):
                w1 = WS1[:, pc % 2, 0, wh, :].rearrange("p (c n) -> p c n", c=NC)
                for c in range(NC):
                    q += 1
                    m = op("pe", lambda e, c=c, w1=w1, xh=xh, q=q: e.matmul(
                        bank(n % 4, 0, 256), w1[:, c, 128 * f:128 * f + 128], XS1[:, xh, c, :],
                        start=(q == 1), stop=(q == 12)), m_sp[pc, 0], m_g.get(n - 4), m_xs, *m_start, inc=(q == 12))
            m_up[n] = m
            m_g[n] = op("act", lambda e: e.activation(
                HF1[:, n % 4, :], bank(n % 4, 0, 256), ACT.Gelu, bias=b1[:, n:n + 1]), m, m_h.get(n - 4), *m_start)
            hi = op("dve", lambda e: e.tensor_copy(HS1[:, n % 4, 0, :], HF1[:, n % 4, :]), m_g[n], m_dn.get(n - 4))
            m_h[n] = op("pool", lambda e: e.tensor_tensor(
                HS1[:, n % 4, 1, :], HF1[:, n % 4, :], HS1[:, n % 4, 0, :].bitcast(F32), ALU.subtract), hi)

        def down1(n):
            pc, f = n // 4, n % 4
            x, fc = n // 16, n % 16
            for i in range(2):
                b = 4 + 2 * (x % 2) + i
                for q, (hh, wh) in enumerate(((0, 0), (0, 1), (1, 0))):
                    w2 = WS1[:, pc % 2, 1, wh, :].rearrange("p (f n) -> p f n", f=4)
                    m = op("pe", lambda e, i=i, b=b, q=q, hh=hh, w2=w2: e.matmul(
                        bank(b), HS1[:, n % 4, hh, 128 * i:128 * i + 128], w2[:, f, :],
                        start=(fc == 0 and q == 0), stop=(fc == 15 and q == 2)),
                        m_h[n], m_sp[pc, 1], m_acc.get((x - 2, i)), inc=(i == 1 and q == 2))
            m_dn[n] = m
            if fc == 15:
                for i in range(2):
                    b = 4 + 2 * (x % 2) + i
                    m_acc[x, i] = op("dve", lambda e, i=i, b=b: e.scalar_tensor_tensor(
                        out=ACC[:, i, :], in0=bank(b), scalar=comb[:, i, x:x + 1], in1=ACC[:, i, :],
                        op0=ALU.mult, op1=ALU.add), m, m_acc.get((x - 1, i)), *m_start)

        split1(0, 0)
        split1(0, 1)
        for n in range(128):
            up1(n)
            pc, f = n // 4, n % 4
            if pc + 1 < NPC and f in (1, 2):
                split1(pc + 1, f - 1)
            if n >= 2:
                down1(n - 2)
        down1(126)
        down1(127)
        K.chained = True
        for i in range(2):
            op("dve", lambda e, i=i: e.bn_stats(st[:, i, :], ACC[:, i, :]))
            m = op("dve", lambda e, i=i: e.bn_aggr(mv[:, i, :], st[:, i, :]))
        op("pool", lambda e: e.tensor_scalar(rstd[:, :], mv[:, :, 1], 1e-5, None, ALU.add), m)
        m = op("pool", lambda e: e.tensor_tensor(rstd[:, :], rstd[:, :], half[:, :], ALU.pow))
        for i in range(2):
            op("dve", lambda e, i=i: e.tensor_scalar(
                ACC[:, i, :], ACC[:, i, :], mv[:, i, 0:1], rstd[:, i:i + 1], ALU.subtract, ALU.mult), m)
            op("dve", lambda e, i=i: e.tensor_tensor(ACC[:, i, :], ACC[:, i, :], lng, ALU.mult), m_ln)
            op("dve", lambda e, i=i: e.tensor_tensor(ACC[:, i, :], ACC[:, i, :], lnb, ALU.add))
            m2 = op("dve", lambda e, i=i: e.tensor_tensor(X[:, i, :], X[:, i, :], ACC[:, i, :], ALU.add))
        m_out = dma(lambda e: e.dma_start(a["out"], X[:, :, :]), "d_out", m2)

        sems = {}
        for s in K.n:
            if s != "sp":
                sems[s] = ctx.enter_context(nc.semaphore("s_" + s))
        block = ctx.enter_context(nc.Block())

        @block.sync
        def _(e):
            K.play("sp", e, sems)
            e.wait_ge(sems["d_out"], m_out[1])

        @block.tensor
        def _(e):
            K.play("pe", e, sems)

        @block.scalar
        def _(e):
            K.play("act", e, sems)

        @block.vector
        def _(e):
            K.play("dve", e, sems)

        @block.gpsimd
        def _(e):
            K.play("pool", e, sems)


def layout(inp):
    f = {k: np.asarray(v) for k, v in inp.items()}

    def rows(w):
        return w.reshape(-1, P, w.shape[-1]).transpose(1, 0, 2)

    def cols(v):
        return v.reshape(-1, P).T

    def flat(*parts):
        return np.ascontiguousarray(np.concatenate([p.reshape(P, -1) for p in parts], axis=1))

    def rep(v):
        return np.broadcast_to(v.reshape(1, -1), (P, v.size))

    ctx = f["ctx_1024"].reshape(NG, GT, NC, P).transpose(0, 3, 2, 1).reshape(NG, P, NC * GT)
    w = f["L0_xattn_W"]
    qkv = f["L1_attn_w_qkv"].reshape(D, H, 3, 32).transpose(0, 2, 1, 3).reshape(D, 3 * D)
    bq = f["L1_attn_b_qkv"].reshape(H, 3, 32).transpose(1, 0, 2).reshape(3, D)
    b0 = f["L0_attn_bqkv"].reshape(3, D)
    w1 = np.concatenate([f["L0_ffn_w1"], f["L0_ffn_ws1"][None]])
    w2 = np.concatenate([f["L0_ffn_w2"], f["L0_ffn_ws2"][None]])
    w3 = np.concatenate([f["L0_ffn_w3"], f["L0_ffn_ws3"][None]])
    l0f = np.stack([flat(rows(w1[e].T), rows(w3[e].T), rows(w2[e].T)) for e in range(17)])
    l1f = []
    for e in range(8):
        for q in range(4):
            l1f.append(flat(rows(f["L1_ffn_w1"][e][:, 512 * q:512 * q + 512]),
                            rows(f["L1_ffn_w2"][e][512 * q:512 * q + 512])))
    return {
        "x": np.ascontiguousarray(f["x"].reshape(2, P, D).transpose(1, 0, 2)),
        "ctx": np.ascontiguousarray(ctx),
        "wkv": flat(rows(f["L1_xattn_Wk"]), rows(f["L1_xattn_Wv"])),
        "l0x": flat(rows(w[:, :D].T), rows(w[:, D:].T)),
        "l0a": flat(rows(f["L0_attn_Wqkv"].T), rows(f["L0_attn_Wo"].T)),
        "l1a": flat(rows(qkv), rows(f["L1_attn_w_o"])),
        "l1x": flat(rows(f["L1_xattn_Wq"]), rows(f["L1_xattn_Wo"])),
        "bcol": flat(cols(b0[0]), cols(b0[1]), cols(f["L1_xattn_bq"]), cols(f["L1_xattn_bk"]), cols(bq[0]), cols(bq[1])),
        "brow": np.stack([f["L0_xattn_b"], b0[2], f["L0_attn_bo"], f["L1_xattn_bv"], f["L1_xattn_bo"], bq[2],
                          f["L1_attn_b_o"]]),
        "l0g": flat(rows(f["L0_ffn_gate_w"].T), rep(f["L0_ffn_gate_bias"])),
        "l0f": l0f,
        "l1g": flat(cols(f["L1_ffn_b1"]), rows(f["L1_ffn_gate_w"]), rep(f["L1_ffn_gate_b"])),
        "l1f": np.stack(l1f),
        "b2": np.ascontiguousarray(f["L1_ffn_b2"]),
        "lngb": np.stack([f["L1_ffn_ln_g"], f["L1_ffn_ln_b"]]),
    }


def kernel(**inputs):
    import concourse.bacc as _bacc
    from concourse.bass_utils import run_bass_kernel_spmd as _run

    arrays = layout(inputs)
    nc = _bacc.Bacc("TRN2", target_bir_lowering=False, num_devices=1)
    aps = {k: nc.dram_tensor(f"in_{k}", v.shape, mybir.dt.from_np(v.dtype), kind="ExternalInput").ap()
           for k, v in arrays.items()}
    aps["out"] = nc.dram_tensor("out_x", (P, 2, D), F32, kind="ExternalOutput").ap()
    build(nc, aps)
    r = _run(nc, [{f"in_{k}": v for k, v in arrays.items()}], core_ids=[0])
    y = r.results[0]["out_x"]
    return np.ascontiguousarray(np.asarray(y).transpose(1, 0, 2)).reshape(1, 256, D)
```

```python
from contextlib import ExitStack

import numpy as np

import concourse.bass as bass
from concourse import mybir

P = 128
F32 = mybir.dt.float32
F32R = mybir.dt.float32r
ALU = mybir.AluOpType
ACT = mybir.ActivationFunctionType
AX = mybir.AxisListType

D = 512
NC = 4
NCTX = 25088
GT = 256
NG = NCTX // GT
NT = NCTX // P
NCH = 4 * NT
NST = (NG - 2) // 3
H = 16
SCALE = float(1.0 / np.sqrt(np.float32(32.0)))
NEG = -1.0e30

C_L0Q, C_L0K, C_L1XQ, C_L1XK, C_L1AQ, C_L1AK = 0, 4, 8, 12, 16, 20
R_L0X, R_L0V, R_L0O, R_XV, R_XO, R_AV, R_AO = range(7)
BSLOT = [0, 1, 2, 3, 0, 1, 2]


CALLS = {
    "matmul": lambda e, a, k: e.matmul(*a, **k),
    "transpose": lambda e, a, k: e.transpose(*a, **k),
    "activation": lambda e, a, k: e.activation(*a, **k),
    "tensor_tensor": lambda e, a, k: e.tensor_tensor(*a, **k),
    "tensor_scalar": lambda e, a, k: e.tensor_scalar(*a, **k),
    "scalar_tensor_tensor": lambda e, a, k: e.scalar_tensor_tensor(*a, **k),
    "tensor_reduce": lambda e, a, k: e.tensor_reduce(*a, **k),
    "tensor_copy": lambda e, a, k: e.tensor_copy(*a, **k),
    "reciprocal": lambda e, a, k: e.reciprocal(*a, **k),
    "memset": lambda e, a, k: e.memset(*a, **k),
    "affine_select": lambda e, a, k: e.affine_select(*a, **k),
    "bn_stats": lambda e, a, k: e.bn_stats(*a, **k),
    "bn_aggr": lambda e, a, k: e.bn_aggr(*a, **k),
    "dma_start": lambda e, a, k: e.dma_start(*a, **k),
}


class Noted:


    def matmul(self, *a, **k):
        return "matmul", a, k

    def transpose(self, *a, **k):
        return "transpose", a, k

    def activation(self, *a, **k):
        return "activation", a, k

    def tensor_tensor(self, *a, **k):
        return "tensor_tensor", a, k

    def tensor_scalar(self, *a, **k):
        return "tensor_scalar", a, k

    def scalar_tensor_tensor(self, *a, **k):
        return "scalar_tensor_tensor", a, k

    def tensor_reduce(self, *a, **k):
        return "tensor_reduce", a, k

    def tensor_copy(self, *a, **k):
        return "tensor_copy", a, k

    def reciprocal(self, *a, **k):
        return "reciprocal", a, k

    def memset(self, *a, **k):
        return "memset", a, k

    def affine_select(self, *a, **k):
        return "affine_select", a, k

    def bn_stats(self, *a, **k):
        return "bn_stats", a, k

    def bn_aggr(self, *a, **k):
        return "bn_aggr", a, k

    def dma_start(self, *a, **k):
        return "dma_start", a, k


class Queues:

    def __init__(self):
        self.q = {e: [] for e in ("pe", "act", "dve", "pool", "sp")}
        self.n = {e: 0 for e in self.q}
        self.seen = {e: {} for e in self.q}
        self.chained = False

    def op(self, eng, fn, *waits, inc=True):
        waits = [w for w in waits if w is not None]
        if self.chained and eng in ("act", "dve", "pool") and self.n[eng]:
            waits.append((eng, self.n[eng]))
        need = []
        for s, v in waits:
            if self.seen[eng].get(s, 0) < v:
                self.seen[eng][s] = v
                need.append((s, v))
        if inc:
            self.n[eng] += 1
        self.q[eng].append((need, fn(Noted()), eng if inc else None, 1))
        return (eng, self.n[eng])

    def dma(self, fn, sem, *waits):
        need = []
        for s, v in [w for w in waits if w is not None]:
            if self.seen["sp"].get(s, 0) < v:
                self.seen["sp"][s] = v
                need.append((s, v))
        self.n[sem] = self.n.get(sem, 0) + 16
        self.q["sp"].append((need, fn(Noted()), sem, 16))
        return (sem, self.n[sem])

    def play(self, eng, e, sems):
        for need, (name, args, kw), sem, by in self.q[eng]:
            for s, v in need:
                e.wait_ge(sems[s], v)
            ins = CALLS[name](e, args, kw)
            if sem is not None:
                ins.then_inc(sems[sem], by)


def build(nc, a):
    K = Queues()
    op, dma = K.op, K.dma
    ctx = ExitStack()
    with ctx:
        def sb(name, shape, dt=F32, over=None):
            return (over or ctx).enter_context(nc.sbuf_tensor(name, shape, dt))

        X = sb("X", [P, 2, D])
        XT = sb("XT", [P, NC, 256])
        BI = sb("BI", [P, 4, D])
        BC = sb("BC", [P, 24])
        ident = sb("ident", [P, P])
        mask0 = sb("mask0", [P, 384])
        mask1 = sb("mask1", [P, 256])
        lt = sb("lt", [P, 256])
        st = sb("st", [P, 2, 6])
        mv = sb("mv", [P, 2, 2])
        rstd = sb("rstd", [P, 2])
        half = sb("half", [P, 2])
        hm = sb("hm", [P, 4])
        small = sb("small", [P, 1024])
        PB = ctx.enter_context(nc.psum_tensor("PB", [P, 8, 512], F32))

        vscr = nc.dram_tensor("v_scr", (2 * NST, P, D), F32, kind="Internal").ap()

        def bank(b, o=0, n=512):
            return PB[:, b, o:o + n]

        def last(eng):
            return (eng, K.n[eng])

        K.chained = True
        kv_life, ffn_life, life = ExitStack(), ExitStack(), ExitStack()
        WKV = sb("WKV", [P, 4, NC, D], F32R, kv_life)
        RAW = sb("RAW", [P, 3, NC * GT], over=kv_life)
        WF = sb("WF", [P, 2, 3, 1536], over=ffn_life)
        W0 = sb("W0", [P, 4096], over=life)
        AR = sb("AR", [P, 12288], over=life)
        early = ExitStack()
        CS = sb("CS", [P, 3, 2, NC, GT], F32R, early)

        m_x = dma(lambda e: e.dma_start(X[:, :, :], a["x"]), "d_x")
        m_bc = dma(lambda e: e.dma_start(BC[:, :], a["bcol"]), "d_bc")

        def load_bias(r, *w):
            s = BSLOT[r]
            return dma(lambda e: e.dma_start(BI[:, s, :], a["brow"][r:r + 1, :].to_broadcast([P, D])),
                       f"d_bi{s}", *w)

        op("pool", lambda e: e.memset(half[:, :], -0.5))
        op("pool", lambda e: e.memset(ident[:, :], 0.0))
        op("pool", lambda e: e.affine_select(out=ident[:, :], in_=ident[:, :], compare_op=ALU.not_equal,
                                             fill=1.0, base=0, pattern=[[-1, P]], channel_multiplier=1))
        op("pool", lambda e: e.memset(mask0[:, :], 0.0))
        op("pool", lambda e: e.affine_select(out=mask0[:, 0:128], in_=mask0[:, 0:128], compare_op=ALU.is_ge,
                                             fill=NEG, base=0, pattern=[[-1, P]], channel_multiplier=1))
        op("pool", lambda e: e.affine_select(out=mask0[:, 128:256], in_=mask0[:, 128:256], compare_op=ALU.is_ge,
                                             fill=NEG, base=-1, pattern=[[1, P]], channel_multiplier=-1))
        op("pool", lambda e: e.affine_select(out=mask0[:, 256:384], in_=mask0[:, 256:384], compare_op=ALU.is_ge,
                                             fill=NEG, base=0, pattern=[[-1, P]], channel_multiplier=1))
        op("pool", lambda e: e.memset(mask1[:, :], 0.0))
        for w in range(2):
            op("pool", lambda e, w=w: e.memset(mask1[0:64, 128 * w + 64:128 * w + 128], NEG))
            op("pool", lambda e, w=w: e.memset(mask1[64:128, 128 * w:128 * w + 64], NEG))
        op("pool", lambda e: e.memset(lt[:, :], 1.0))
        op("pool", lambda e: e.affine_select(out=lt[:, :].rearrange("p (a b) -> p a b", a=16),
                                             in_=lt[:, :].rearrange("p (a b) -> p a b", a=16),
                                             compare_op=ALU.is_gt, fill=0.0, base=0,
                                             pattern=[[1, 16], [-1, 16]], channel_multiplier=0))
        op("pool", lambda e: e.memset(hm[:, :], 0.0))
        for s in range(4):
            op("pool", lambda e: e.memset(hm[32 * s:32 * s + 32, s:s + 1], 1.0))
        m_const = last("pool")

        def layernorm(XN, *w):
            for i in range(2):
                op("dve", lambda e, i=i: e.bn_stats(st[:, i, :], X[:, i, :]), *w)
                m = op("dve", lambda e, i=i: e.bn_aggr(mv[:, i, :], st[:, i, :]))
            op("pool", lambda e: e.tensor_scalar(rstd[:, :], mv[:, :, 1], 1e-5, None, ALU.add), m)
            m = op("pool", lambda e: e.tensor_tensor(rstd[:, :], rstd[:, :], half[:, :], ALU.pow))
            for i in range(2):
                m = op("dve", lambda e, i=i: e.tensor_scalar(
                    XN[:, i, :], X[:, i, :], mv[:, i, 0:1], rstd[:, i:i + 1], ALU.subtract, ALU.mult), m)
            return m

        def transpose_to(dst, src, m_src, *w, roll=0):
            for c in range(NC):
                for i in range(2):
                    m = op("pe", lambda e, c=c, i=i: e.transpose(
                        bank(c // 2, 256 * (c % 2) + 128 * i, 128), src[:, i, 128 * c:128 * c + 128], ident[:, :]),
                        m_src, m_const, *w, inc=(c % 2 == 1 and i == 1))
                if c % 2:
                    b = c // 2
                    d = dst[:, 2 * b:2 * b + 2, :]
                    s = bank(b).rearrange("p (c i) -> p c i", c=2)
                    if not roll:
                        out = op("act" if b else "dve", lambda e, d=d, s=s, b=b: (
                            e.activation(d, s, ACT.Copy) if b else e.tensor_copy(d, s)), m)
                    else:
                        op("dve", lambda e, d=d, s=s: e.tensor_copy(d[:, :, 0:256 - roll], s[:, :, roll:256]), m)
                        out = op("dve", lambda e, d=d, s=s: e.tensor_copy(d[:, :, 256 - roll:256], s[:, :, 0:roll]))
                    if not b:
                        first = out
            return [first, out]

        sums = small[:, 0:4 * NG]
        m_red, m_ld, m_used = [], [], {}

        def load_sums(n):
            m_ld.append(dma(lambda e: e.dma_start(
                AR[:, 2048 * (n % 4):2048 * (n % 4) + 2048].rearrange("p (g f) -> p g f", g=2),
                a["ctx"][2 * n:2 * n + 2].rearrange("g p f -> p g f")), f"d_c{n % 4}",
                m_red[n - 4] if n >= 4 else None, m_used.get(n - 4)))

        wraw = WF[:, 0].rearrange("p m f -> p (m f)")[:, 0:2048]
        VR = RAW[:, :, :].rearrange("p r f -> p (r f)").rearrange("p (r n) -> p r n", r=6)
        m_split, m_vk, m_vb, m_vst, m_pool = {}, {}, {}, {}, None

        def load_wkv(m, *w):
            return dma(lambda e: e.dma_start(wraw, a["wkv"][:, 2048 * m:2048 * m + 2048]),
                       "d_f0", *w)

        def split_wkv(m, c, eng, m_w):
            z = slice(512 * c, 512 * c + 512)
            hi = op("act", lambda e: e.activation(WKV[:, 2 * m, c, :], wraw[:, z], ACT.Copy), m_w)
            return op(eng, lambda e: e.tensor_tensor(
                WKV[:, 2 * m + 1, c, :], wraw[:, z], WKV[:, 2 * m, c, :].bitcast(F32), ALU.subtract), hi)

        m_wv = load_wkv(1)
        m_bi = {R_XV: load_bias(R_XV)}
        for n in range(4):
            load_sums(n)
        XN = AR[:, 9216:10240].rearrange("p (i n) -> p i n", i=2)
        m_wvs = [split_wkv(1, c, "pool" if c % 2 else "dve", m_wv) for c in range(NC)]
        m = layernorm(XN, m_x)
        m_xt = transpose_to(XT, XN, m)
        K.chained = False

        def early_split(q):
            g = 3 * q + 2
            src = AR[:, 2048 * ((g // 2) % 4) + 1024 * (g % 2):][:, 0:1024]
            d = [CS[:, q % 3, h].rearrange("p c j -> p (c j)") for h in range(2)]
            hi = op("act", lambda e: e.activation(d[0], src, ACT.Copy), m_ld[g // 2], m_vk.get(2 * (q - 3) + 1))
            m_used[g // 2] = m_split[q] = op("pool", lambda e: e.tensor_tensor(d[1], src, d[0].bitcast(F32), ALU.subtract), hi)

        def early_v(r):
            q, j = r // 2, 128 * (r % 2)
            n = 0
            for xh, wh in ((0, 0), (0, 1), (1, 0)):
                for c in range(NC):
                    n += 1
                    m = op("pe", lambda e: e.matmul(
                        bank(5 + r % 3), CS[:, q % 3, xh, c, j:j + 128], WKV[:, 2 + wh, c, :],
                        start=(n == 1), stop=(n == 12)), m_split[q], m_vb.get(r - 3), *m_wvs, inc=(n == 12))
            m_vk[r] = m

        def early_out(r):
            m_vb[r] = op("dve", lambda e: e.tensor_tensor(VR[:, r % 6], bank(5 + r % 3), BI[:, BSLOT[R_XV], :], ALU.add),
                         m_vk[r], m_bi[R_XV], m_vst.get(r - 6))

        def early_store(r):
            m_vst[r] = dma(lambda e: e.dma_start(vscr[r], VR[:, r % 6]), f"d_v{r % 6}", m_vb[r])

        def pair_v(n):
            return [2 * q + j for q in range(NST) for j in range(2) if (3 * q + 2) // 2 == n]

        for n in range(NG // 2 + 2):
            if n < NG // 2:
                m_red.append(op("dve", lambda e: e.tensor_reduce(
                    sums[:, 8 * n:8 * n + 8], AR[:, 2048 * (n % 4):2048 * (n % 4) + 2048].rearrange("p (g f) -> p g f", f=GT),
                    axis=AX.X, op=ALU.add), m_ld[n]))
                for r in pair_v(n)[0:2:2]:
                    early_split(r // 2)
            for r in pair_v(n - 1):
                early_out(r)
            for r in pair_v(n):
                early_v(r)
            for r in pair_v(n - 2):
                early_store(r)
            if n + 4 < NG // 2:
                load_sums(n + 4)
            if n == 6:
                m_wk = load_wkv(0, *m_wvs)
            if n in (12, 15, 18, 21):
                m_wsplit = split_wkv(0, (n - 12) // 3, "pool", m_wk)
            if n == 26:
                m_l0x = dma(lambda e: e.dma_start(W0[:, :], a["l0x"]), "d_w0")
                m_bi.update({r: load_bias(r) for r in (R_L0X, R_L0V, R_L0O)})
            if n == 36:
                w0 = W0[:, :].rearrange("p (m c n) -> p m c n", m=2, c=NC)
                for i in range(2):
                    for c in range(NC):
                        m_p1 = op("pe", lambda e: e.matmul(
                            bank(2 + i), XT[:, c, 128 * i:128 * i + 128], w0[:, 0, c, :],
                            start=(c == 0), stop=(c == NC - 1)), *m_xt, m_l0x, inc=(c == NC - 1))
            if n == 42:
                for i in range(2):
                    mb = op("dve", lambda e: e.tensor_tensor(X[:, i, :], X[:, i, :], BI[:, 0, :], ALU.add),
                            m_bi[R_L0X])
                    m_xb = op("dve", lambda e: e.tensor_tensor(X[:, i, :], X[:, i, :], bank(2 + i), ALU.add), m_p1, mb)
        K.chained = True
        early.close()
        WA = sb("WA", [P, 8192], over=life)
        m_wl0 = dma(lambda e: e.dma_start(WA[:, :], a["l0a"]), "d_wa", last("pe"), last("act"), last("pool"))
        csum = small[:, 400:404]
        op("dve", lambda e: e.tensor_reduce(csum, sums.rearrange("p (g c) -> p c g", c=NC), axis=AX.X, op=ALU.add))
        SBC = AR[:, 10240:10752].rearrange("p (c i) -> p c i", c=NC)
        m_sbc = op("dve", lambda e: e.tensor_scalar(SBC, csum.unsqueeze(2).to_broadcast([P, NC, P]),
                                                    1.0 / NCTX, None, ALU.mult))
        for c in range(NC):
            m = op("pe", lambda e: e.matmul(bank(4), SBC[:, c, :], w0[:, 1, c, :], start=(c == 0), stop=(c == NC - 1)),
                   m_sbc, inc=(c == NC - 1))
        for i in range(2):
            op("dve", lambda e: e.tensor_tensor(X[:, i, :], X[:, i, :], bank(4), ALU.add), m)
        m_bi[R_XO] = load_bias(R_XO, m_xb)

        m_v0 = [last("pe"), m_wsplit]

        def self_attention(WA, AR, QM, cq, ck, rv, ro, m_w, mask, blocks, roll):
            NB = len(blocks)
            W = 128 * NB
            XN = AR[:, 9216:9216 + 1024].rearrange("p (i n) -> p i n", i=2)
            QT = AR[:, 0:0 + 1024].rearrange("p (c i) -> p c i", c=NC)
            KT = AR[:, 1024:1024 + 1024].rearrange("p (c i) -> p c i", c=NC)
            V = AR[:, 2048:2048 + 1024].rearrange("p (i n) -> p i n", i=2)
            SM = AR[:, 3072:3072 + 12 * W].rearrange("p (b s w) -> p b s w", b=3, s=4)
            PT = AR[:, 7680:7680 + 4 * W].rearrange("p (s w) -> p s w", s=4)
            DG = AR[:, 9216:9216 + 2048].rearrange("p (b s i q) -> p b s i q", b=2, s=4, i=2)
            ATT = AR[:, 11264:11264 + 1024].rearrange("p (c i) -> p c i", c=NC)
            wq = WA[:, 0:6144].rearrange("p (c n) -> p c n", c=NC)
            wo = WA[:, 6144:8192].rearrange("p (c n) -> p c n", c=NC)
            QM = QM.rearrange("p (b s i) -> p b s i", b=2, s=4)
            nm = small[:, 0:16].rearrange("p (b s i) -> p b s i", b=2, i=2)
            su = small[:, 16:48].rearrange("p (h i) -> p h i", i=2)
            rc = small[:, 48:80].rearrange("p (h i) -> p h i", i=2)
            m = layernorm(XN, last("pe"))
            m_xt = transpose_to(XT, XN, m, roll=roll)
            for m8 in range(8):
                b = 2 + m8 // 2
                o = 256 * (m8 % 2)
                for c in range(NC):
                    m = op("pe", lambda e, m8=m8, c=c, b=b, o=o: e.matmul(
                        bank(b, o, 256), wq[:, c, 128 * m8:128 * m8 + 128], XT[:, c, :],
                        start=(c == 0), stop=(c == NC - 1)), *m_xt, m_w, inc=(c == NC - 1))
                if m8 % 2:
                    for z in (m8 - 1, m8):
                        oz = 256 * (z % 2)
                        if z < 4:
                            m_q = op("dve", lambda e, z=z, b=b, oz=oz: e.tensor_scalar(
                                QT[:, z, :], bank(b, oz, 256), BC[:, cq + z:cq + z + 1], SCALE, ALU.add, ALU.mult),
                                m, m_bc)
                        else:
                            m_q = op("dve", lambda e, z=z, b=b, oz=oz: e.tensor_scalar(
                                KT[:, z - 4, :], bank(b, oz, 256), BC[:, ck + z - 4:ck + z - 3], None, ALU.add),
                                m, m_bc)
            for i in range(2):
                for c in range(NC):
                    m = op("pe", lambda e, i=i, c=c: e.matmul(
                        bank(6 + i), XT[:, c, 128 * i:128 * i + 128], wq[:, c, 1024:1536],
                        start=(c == 0), stop=(c == NC - 1)), inc=(c == NC - 1))
                m_v = op("dve", lambda e, i=i: e.tensor_tensor(V[:, i, :], bank(6 + i), BI[:, BSLOT[rv], :], ALU.add),
                         m, m_bi[rv])
            for i in range(2):
                m_xb = op("dve", lambda e, i=i: e.tensor_tensor(X[:, i, :], X[:, i, :], BI[:, BSLOT[ro], :], ALU.add),
                          m_bi[ro])
            m_sm, m_tr, m_pt = {}, {}, {}
            rng = {i: [z for z, (q, _) in enumerate(blocks) if q == i] for i in range(2)}
            m_ex = {}

            K.chained = False

            def single_heads(c):
                m_qm[c] = op("pool", lambda e: e.tensor_tensor(
                    QM[:, c % 2], QT[:, c, :].unsqueeze(1).to_broadcast([P, 4, 256]),
                    hm[:, :].unsqueeze(2).to_broadcast([P, 4, 256]), ALU.mult), m_q, m_sc.get(c - 2))

            def scores(c):
                for s in range(4):
                    for i in range(2):
                        z0, nz = rng[i][0], len(rng[i])
                        j0 = blocks[z0][1]
                        m = op("pe", lambda e: e.matmul(
                            bank(s, 128 * z0, 128 * nz), QM[:, c % 2, s, 128 * i:128 * i + 128],
                            KT[:, c, 128 * j0:128 * (j0 + nz)], start=True, stop=True),
                            m_q, m_qm[c], m_sm.get(c - 1), inc=(s == 3 and i == 1))
                m_sc[c] = m
                if c + 2 < NC:
                    single_heads(c + 2)
                b = c % 3
                m_sm[c] = op("dve", lambda e: e.tensor_tensor(
                    SM[:, b], PB[:, 0:4, 0:W], mask[:, 0:W].unsqueeze(1).to_broadcast([P, 4, W]), ALU.add),
                    m, m_const, m_tr.get(c - 3))
                for i in range(2):
                    z0, nz = rng[i][0], len(rng[i])
                    m = op("dve", lambda e: e.tensor_reduce(
                        nm[:, c % 2, :, i], SM[:, b, :, 128 * z0:128 * (z0 + nz)], axis=AX.X, op=ALU.max, negate=True),
                        m_sm[c], m_ex.get(c - 2))
                for s in range(4):
                    for i in range(2):
                        z0, nz = rng[i][0], len(rng[i])
                        v = SM[:, b, s, 128 * z0:128 * (z0 + nz)]
                        m_ex[c] = op("act", lambda e: e.activation(
                            v, v, ACT.Exp, bias=nm[:, c % 2, s, i:i + 1], accum_out=su[:, 4 * c + s, i:i + 1]), m)

            def diagonals(c):
                m = op("dve", lambda e: e.reciprocal(rc[:, 4 * c:4 * c + 4], su[:, 4 * c:4 * c + 4]), m_ex[c])
                d = DG[:, c % 2].rearrange("p s i q -> p (s i) q")
                r = rc[:, 4 * c:4 * c + 4].rearrange("p s i -> p (s i)")
                m_dg[c] = op("pool", lambda e: e.tensor_tensor(
                    d, ident[:, :].unsqueeze(1).to_broadcast([P, 8, P]), r.unsqueeze(2).to_broadcast([P, 8, P]),
                    ALU.mult), m, m_tr.get(c - 2), m_q)

            def turn(c):
                for s in range(4):
                    pb = 4 + s % 2
                    for z, (i, j) in enumerate(blocks):
                        m = op("pe", lambda e: e.matmul(
                            bank(pb, 128 * z, 128), SM[:, c % 3, s, 128 * z:128 * z + 128], DG[:, c % 2, s, i, :],
                            start=True, stop=True), m_dg[c], m_pt.get(4 * c + s - 2), inc=(z == NB - 1))
                    m_tr[c] = m
                    m_pt[4 * c + s] = op("dve", lambda e: e.tensor_copy(PT[:, s, :], bank(pb, 0, W)), m,
                                         m_mix.get(c - 1))

            def mix(c):
                for z, (i, j) in enumerate(blocks):
                    for s in range(4):
                        h = 4 * c + s
                        m = op("pe", lambda e: e.matmul(
                            PB[32 * s:32 * s + 32, 6 + c % 2, 128 * i:128 * i + 128], V[:, j, 32 * h:32 * h + 32],
                            PT[:, s, 128 * z:128 * z + 128], start=(z == rng[i][0]), stop=(z == rng[i][-1]),
                            skip_group_check=True),
                            m_pt[4 * c + 3], m_pt[4 * c + 2], m_v, m_at.get(c - 2), inc=(z == NB - 1 and s == 3))
                m_mix[c] = m
                n = 256 - roll
                m_at[c] = op("dve", lambda e: e.tensor_copy(ATT[:, c, roll:256], bank(6 + c % 2, 0, n)), m)
                if roll:
                    m_at[c] = op("dve", lambda e: e.tensor_copy(ATT[:, c, 0:roll], bank(6 + c % 2, n, roll)))

            m_dg, m_mix, m_at, m_qm, m_sc = {}, {}, {}, {}, {}
            single_heads(0)
            single_heads(1)
            scores(0)
            diagonals(0)
            scores(1)
            for c in range(NC):
                turn(c)
                if c + 1 < NC:
                    diagonals(c + 1)
                if c + 2 < NC:
                    scores(c + 2)
                mix(c)
            K.chained = True
            m_at = m_at.values()
            for i in range(2):
                for c in range(NC):
                    m = op("pe", lambda e, i=i, c=c: e.matmul(
                        bank(2 + i), ATT[:, c, 128 * i:128 * i + 128], wo[:, c, :],
                        start=(c == 0), stop=(c == NC - 1)), *m_at, inc=(c == NC - 1))
                op("dve", lambda e, i=i: e.tensor_tensor(X[:, i, :], X[:, i, :], bank(2 + i), ALU.add), m)
            return m_xb

        m_hf, m_acc, m_h, m_w, m_sp, m_dn, m_up = ({} for _ in range(7))

        def load0(x, *w):
            m_w[x] = dma(lambda e: e.dma_start(WF[:, x % 2].rearrange("p m f -> p (m f)"), a["l0f"][x]),
                         f"d_f{x % 2}", m_sp.get((x - 2, 2)), *w)

        load0(0, *m_v0)
        load0(1, *m_v0)

        m_xb = self_attention(WA, AR, W0[:, 0:2048], C_L0Q, C_L0K, R_L0V, R_L0O, m_wl0, mask0, [(0, 0), (1, 0), (1, 1)], 0)
        m_bi[R_AV] = load_bias(R_AV, m_xb)
        m_bi[R_AO] = load_bias(R_AO, m_xb)
        life.close()

        def ranks(dst, v, E, n, m_l):
            g, t = (small[:, o:o + n * E * E].rearrange("p (g a b) -> p g a b", g=n, a=E) for o in (512, 768))
            vv = v.rearrange("p (g a) -> p g a", g=n)
            o = vv.unsqueeze(2).to_broadcast([P, n, E, E])
            s = vv.unsqueeze(3).to_broadcast([P, n, E, E])
            l = lt[:, :].rearrange("p (a b) -> p a b", a=16)[:, 0:E, 0:E].unsqueeze(1).to_broadcast([P, n, E, E])
            op("dve", lambda e: e.tensor_tensor(g, o, s, ALU.is_equal))
            op("dve", lambda e: e.tensor_tensor(g, g, l, ALU.mult), m_l)
            op("dve", lambda e: e.tensor_tensor(t, o, s, ALU.is_gt))
            op("dve", lambda e: e.tensor_tensor(g, g, t, ALU.add))
            op("dve", lambda e: e.tensor_reduce(dst.rearrange("p (g a) -> p g a", g=n), g, axis=AX.X, op=ALU.add))

        life = ExitStack()
        WS = sb("WS", [P, 2, 3, 2, 1536], F32R, life)
        XS = sb("XS", [P, 2, NC, 256], F32R, life)
        HS = sb("HS", [P, 2, 3, 2, 256], F32R, life)
        HF = sb("HF", [P, 2, 3, 256], over=life)
        XNF = HF[:, :, :, :].rearrange("p b k i -> p (b k i)")[:, 0:1024].rearrange("p (i n) -> p i n", i=2)
        gw = small[:, 0:64].rearrange("p (c n) -> p c n", c=NC)
        m = layernorm(XNF, last("pe"))
        gb = small[:, 64:80]
        m_gw = dma(lambda e: e.dma_start(small[:, 0:80], a["l0g"]), "d_g", last("dve"), last("act"))
        m_xt = transpose_to(XT, XNF, m)
        comb = small[:, 80:112].rearrange("p (i n) -> p i n", i=2)
        v, rk, t16, sc = (small[:, o:o + 32] for o in (224, 256, 288, 320))
        gs, gm, t1 = small[:, 352:360], small[:, 360:368], small[:, 368:370]
        m_raw, m_lo = {}, {}

        def load_ctx(g):
            m_raw[g] = dma(lambda e: e.dma_start(RAW[:, g % 3, :], a["ctx"][g]), f"d_c{g % 3}", m_lo.get(g - 3),
                           *m_vst.values())

        for g in range(3):
            load_ctx(g)
        split_xt = lambda XS: (
            op("dve", lambda e: e.tensor_copy(XS[:, 0], XT[:, :, :]), *m_xt),
            op("dve", lambda e: e.tensor_tensor(XS[:, 1], XT[:, :, :], XS[:, 0].bitcast(F32), ALU.subtract)))[1]
        m_xs = split_xt(XS)
        m_start = [last("pe"), last("dve"), last("act")]
        K.chained = False
        def split0(x, m):
            r = x % 2
            hi = op("act", lambda e: e.activation(WS[:, r, m, 0, :], WF[:, r, m, :], ACT.Copy), m_w[x],
                    (m_up if m < 2 else m_dn).get(x - 2), *m_start)
            m_sp[x, m] = op("dve", lambda e: e.tensor_tensor(
                WS[:, r, m, 1, :], WF[:, r, m, :], WS[:, r, m, 0, :].bitcast(F32), ALU.subtract), hi)
            if m == 2 and x + 2 < 17:
                load0(x + 2)

        def up0(x, k):
            r, n = x % 2, 3 * x + k
            for u in range(2):
                q = 0
                for wh, xh in ((0, 0), (0, 1), (1, 0)):
                    w = WS[:, r, u, wh, :].rearrange("p (c n) -> p c n", c=NC)
                    for c in range(NC):
                        q += 1
                        m = op("pe", lambda e, w=w, c=c, xh=xh, q=q, u=u: e.matmul(
                            bank(k, 256 * u, 256), w[:, c, 128 * k:128 * k + 128], XS[:, xh, c, :],
                            start=(q == 1), stop=(q == 12)), m_sp[x, u], m_hf.get(n - 3), m_xs, inc=(u == 1 and q == 12))
            m_up[x] = m
            ms = op("act", lambda e: e.activation(HF[:, 0, k, :], bank(k, 0, 256), ACT.Silu), m, m_hf.get(n - 3),
                    *m_start)
            m_hf[n] = op("dve", lambda e: e.tensor_tensor(
                HF[:, 1, k, :], HF[:, 0, k, :], bank(k, 256, 256), ALU.mult), ms, m_h.get(n - 3))
            hi = op("dve", lambda e: e.tensor_copy(HS[:, r, k, 0, :], HF[:, 1, k, :]), m_hf[n], m_dn.get(x - 2))
            m_h[n] = op("pool", lambda e: e.tensor_tensor(
                HS[:, r, k, 1, :], HF[:, 1, k, :], HS[:, r, k, 0, :].bitcast(F32), ALU.subtract), hi)

        def down0(x, i):
            r = x % 2
            b = 4 + 2 * r + i
            steps = [(hh, wh, k) for k in range(3) for hh, wh in ((0, 0), (0, 1), (1, 0))]
            for q, (hh, wh, k) in enumerate(steps):
                w = WS[:, r, 2, wh, :].rearrange("p (k n) -> p k n", k=3)
                m = op("pe", lambda e, hh=hh, w=w, k=k, q=q: e.matmul(
                    bank(b), HS[:, r, k, hh, 128 * i:128 * i + 128], w[:, k, :], start=(q == 0), stop=(q == 8)),
                    m_h[3 * x + k], m_sp[x, 2], m_acc.get((x - 2, i)), inc=(q == 8))
            s = comb[:, i, x:x + 1] if x < 16 else 1.0
            m_acc[x, i] = op("dve", lambda e: e.scalar_tensor_tensor(
                out=X[:, i, :], in0=bank(b), scalar=s, in1=X[:, i, :], op0=ALU.mult, op1=ALU.add),
                m, m_acc.get((x - 1, i)), m_cb, *m_start)
            m_dn[x] = m

        for m in range(3):
            split0(0, m)
        up0(0, 0)
        K.chained = True
        for i in range(2):
            for c in range(NC):
                m = op("pe", lambda e, i=i, c=c: e.matmul(bank(3, 16 * i, 16), XT[:, c, 128 * i:128 * i + 128],
                                                          gw[:, c, :], start=(c == 0), stop=(c == NC - 1)),
                       *m_xt, m_gw, inc=(c == NC - 1))
        m = op("act", lambda e: e.activation(sc, bank(3, 0, 32), ACT.Sigmoid), m)
        v3, t3, s3 = (z.rearrange("p (i n) -> p i n", i=2) for z in (v, t16, sc))
        v4, t4 = (z.rearrange("p (g a) -> p g a", g=8) for z in (v, t16))
        gmb = gm.unsqueeze(2).to_broadcast([P, 8, 4])
        op("dve", lambda e: e.tensor_tensor(v3, s3, gb.unsqueeze(1).to_broadcast([P, 2, 16]), ALU.add), m)
        ranks(rk, v, 4, 8, m_const)
        op("dve", lambda e: e.tensor_scalar(t16, rk, 2.0, None, ALU.is_lt))
        op("dve", lambda e: e.tensor_tensor(t16, t16, v, ALU.mult))
        op("dve", lambda e: e.tensor_reduce(gs, t4, axis=AX.X, op=ALU.add))
        ranks(gm, gs, 4, 2, m_const)
        op("dve", lambda e: e.tensor_scalar(gm, gm, 2.0, None, ALU.is_lt))
        op("dve", lambda e: e.tensor_tensor(v4, v4, gmb, ALU.mult))
        op("dve", lambda e: e.tensor_scalar(t4, gmb, -1.0, 1.0e30, ALU.add, ALU.mult))
        op("dve", lambda e: e.tensor_tensor(v, v, t16, ALU.add))
        for i in range(2):
            ranks(rk[:, 16 * i:16 * i + 16], v[:, 16 * i:16 * i + 16], 16, 1, m_const)
        op("dve", lambda e: e.tensor_scalar(t16, rk, 4.0, None, ALU.is_lt))
        op("dve", lambda e: e.tensor_tensor(t16, t16, sc, ALU.mult))
        op("dve", lambda e: e.tensor_reduce(t1, t3, axis=AX.X, op=ALU.add))
        op("dve", lambda e: e.tensor_scalar(t1, t1, 1e-20, None, ALU.add))
        op("dve", lambda e: e.reciprocal(t1, t1))
        op("dve", lambda e: e.scalar_tensor_tensor(out=comb, in0=t3, scalar=2.5,
                                                   in1=t1.unsqueeze(2).to_broadcast([P, 2, 16]),
                                                   op0=ALU.mult, op1=ALU.mult))
        m_cb = last("dve")
        K.chained = False
        for x in range(17):
            for k in range(3):
                if x or k:
                    up0(x, k)
                if x and k:
                    down0(x - 1, k - 1)
                if x + 1 < 17:
                    split0(x + 1, k)
        down0(16, 0)
        down0(16, 1)
        K.chained = True
        life.close()
        ffn_life.close()

        life = ExitStack()
        CTX = sb("CTX", [P, 3, 2, NC, GT], F32R, life)
        KHL = sb("KHL", [P, 2, 2, NC, GT], F32R, life)
        STK = sb("STK", [P, 2, 4, NC, GT], F32R, life)
        QS = sb("QS", [P, 4, NC, 256], F32R, life)
        V = sb("V", [P, 4, D], over=life)
        VS = sb("VS", [P, 4, P], over=life)
        EE = sb("EE", [P, 4, 4, 256], over=life)
        OT = sb("OT", [P, NC, 256], over=life)
        WO = sb("WO", [P, NC, D], over=life)
        raw = lambda r: RAW[:, r, :]
        wq = EE[:, 0:2].rearrange("p b s i -> p (b s i)").rearrange("p (c n) -> p c n", c=NC)
        XNX = EE[:, 2].rearrange("p s i -> p (s i)").rearrange("p (i n) -> p i n", i=2)
        qf = EE[:, 3].rearrange("p c i -> p (c i)")
        QHL = sb("QHL", [P, 2, NC, 256], F32R, life)
        wo = WO
        m_end = [last("pe"), last("dve"), last("act"), last("pool")]
        m_wx = dma(lambda e: e.dma_start(wq, a["l1x"][:, 0:2048].rearrange("p (c n) -> p c n", c=NC)), "d_w0", *m_end)
        m_wo = dma(lambda e: e.dma_start(WO[:, :, :], a["l1x"][:, 2048:4096].rearrange("p (c n) -> p c n", c=NC)),
                   "d_x", *m_end)
        def stack(dst, src, kinds, sem, *w):
            for s in range(4):
                for q in range(4):
                    m = dma(lambda e, s=s, q=q: e.dma_start(
                        dst[32 * q:32 * q + 32, s, :, :].bitcast(F32),
                        src[32 * s:32 * s + 32, kinds[q], :, :].bitcast(F32)), sem, *w)
            return m

        K.chained = False
        nm = small[:, 0:16].rearrange("p (b s) -> p b s", b=4)
        su = small[:, 16:32].rearrange("p (b s) -> p b s", b=4)
        rc = small[:, 32:48].rearrange("p (b s) -> p b s", b=4)
        m_khi, m_klo, m_kp, m_vp, m_vev, m_vs, m_ex, m_mx, m_rc, m_pv, m_s = ({} for _ in range(11))

        def split_ctx(g):
            b = g % 3
            hi = op("dve", lambda e: e.tensor_copy(CTX[:, b, 0, :, :].rearrange("p c j -> p (c j)"), raw(g % 3)),
                        m_raw[g], m_vp.get(2 * (g - 3) + 1), m_kp.get((g - 3, 3)))
            m_lo[g] = op("pool" if g > 1 else "dve", lambda e: e.tensor_tensor(
                CTX[:, b, 1, :, :].rearrange("p c j -> p (c j)"), raw(g % 3),
                CTX[:, b, 0, :, :].rearrange("p c j -> p (c j)").bitcast(F32), ALU.subtract), hi)
            if g + 3 < NG:
                load_ctx(g + 3)

        def project_k(g, ch, kb=4, part=(0, 12)):
            b = g % 3
            steps = [(wh, xh, c) for wh, xh in ((0, 0), (0, 1), (1, 0)) for c in range(NC)]
            for n in range(*part):
                wh, xh, c = steps[n]
                m = op("pe", lambda e: e.matmul(
                    bank(kb, 0, GT), WKV[:, wh, c, 128 * ch:128 * ch + 128], CTX[:, b, xh, c, :],
                    start=(n == 0), stop=(n == 11)), m_lo[g], m_kbank.get(kb), inc=(n == 11))
            m_kp[g, ch] = m

        m_kbank = {}
        m_q = None
        m_stk = {}

        def stack_k(g):
            m_stk[g] = stack(STK[:, g % 2], KHL[:, g % 2], (0, 1, 0, 1), f"d_s{g % 2}", m_klo[g, 3],
                             m_s.get((8 * (g - 2) + 7, 1)))


        def evac_k_hi(g, ch, kb=4):
            m_khi[g, ch] = op("act", lambda e: e.activation(
                KHL[:, g % 2, 0, ch, :], bank(kb, 0, GT), ACT.Identity, bias=BC[:, C_L1XK + ch:C_L1XK + ch + 1]),
                m_kp[g, ch], m_stk.get(g - 2))

        def evac_k_lo(g, ch, kb=4):
            m_kbank[kb] = m_klo[g, ch] = op("dve", lambda e: e.scalar_tensor_tensor(
                out=KHL[:, g % 2, 1, ch, :], in0=bank(kb, 0, GT), scalar=BC[:, C_L1XK + ch:C_L1XK + ch + 1],
                in1=KHL[:, g % 2, 0, ch, :].bitcast(F32), op0=ALU.add, op1=ALU.subtract), m_khi[g, ch])

        def v_tile(n):
            return 6 * (n // 4) + n % 4

        def project_v(n, part):
            t = v_tile(n)
            g, b, j = t // 2, (t // 2) % 3, 128 * (t % 2)
            steps = [(xh, wh, c) for xh, wh in ((0, 0), (0, 1), (1, 0)) for c in range(NC)]
            for z in range(4 * part, 4 * part + 4):
                xh, wh, c = steps[z]
                m = op("pe", lambda e: e.matmul(
                    bank(5), CTX[:, b, xh, c, j:j + 128], WKV[:, 2 + wh, c, :],
                    start=(z == 0), stop=(z == 11)), m_lo[g], m_vbank[0], m_pro, inc=(z == 11))
            m_vp[t] = m

        m_vbank = [None]

        def evac_v(n):
            t = v_tile(n)
            m_vbank[0] = m_vev[t] = op("dve", lambda e: e.tensor_tensor(
                V[:, t % 4, :], bank(5), BI[:, BSLOT[R_XV], :], ALU.add),
                m_vp[t], m_vs.get(4 * (t - 4) + 3), m_bi[R_XV])

        def fetch_v(t):
            r = 2 * (t // 6) + t % 2
            m_vev[t] = dma(lambda e: e.dma_start(V[:, t % 4, :], vscr[r]), f"d_u{t % 2}", m_vst[r],
                           m_vs.get(4 * (t - 4) + 3), *(m_end if t < 6 else ()))

        def scores(k, half):
            t, c = k // 4, k % 4
            g, b, j = t // 2, (t // 2) % 2, 128 * (t % 2)
            for s in (2 * half, 2 * half + 1):
                o = bank(2 * (k % 2) + half, 256 * (s % 2), 256)
                m = op("pe", lambda e: e.matmul(
                    o, STK[:, b, s, c, j:j + 128], QS[:, s, c, :], start=True, stop=True),
                    m_stk[g], m_ex.get((k - 2, half)), m_pro, m_q, inc=(s % 2 == 1))
            m_s[k, half] = m

        def softmax(k, half):
            b = k % 4
            pb = 2 * (k % 2) + half
            z = slice(2 * half, 2 * half + 2)
            m_mx[k, half] = op("dve", lambda e: e.tensor_reduce(
                nm[:, b, z], bank(pb).rearrange("p (s i) -> p s i", s=2), axis=AX.X, op=ALU.max, negate=True),
                m_s[k, half], m_ex.get((k - 4, half)))
            for s in (2 * half, 2 * half + 1):
                m = op("act", lambda e: e.activation(
                    EE[:, b, s, :], bank(pb, 256 * (s % 2), 256), ACT.Exp, bias=nm[:, b, s:s + 1],
                    accum_out=su[:, b, s:s + 1]), m_mx[k, half], m_pv.get(k - 4), m_rc.get(k - 4), inc=(s % 2 == 1))
            m_ex[k, half] = m

        def scale_v(k):
            b, t, c = k % 4, k // 4, k % 4
            m_rc[k] = op("dve", lambda e: e.reciprocal(rc[:, b, :], su[:, b, :]), m_ex[k, 1], m_vs.get(k - 4))
            m_vs[k] = op("pool", lambda e: e.tensor_tensor(
                VS[:, b, :].rearrange("p (s d) -> p s d", s=4),
                V[:, t % 4, 128 * c:128 * c + 128].rearrange("p (s d) -> p s d", s=4),
                rc[:, b, :].unsqueeze(2).to_broadcast([P, 4, 32]), ALU.mult), m_rc[k], m_pv.get(k - 4), m_vev[t])

        def mix(k):
            t, c, b = k // 4, k % 4, k % 4
            for s in range(4):
                m = op("pe", lambda e, s=s: e.matmul(
                    PB[32 * s:32 * s + 32, 6 + c // 2, 256 * (c % 2):256 * (c % 2) + 256],
                    VS[:, b, 32 * s:32 * s + 32], EE[:, b, s, :],
                    start=(t == 0 and c % 2 == 0), stop=(t == NT - 1), skip_group_check=True),
                    m_vs[k], m_ex[k, 1], inc=(s == 3))
            m_pv[k] = m

        def prologue_k(g):
            for ch, kb in enumerate((6, 2, 3, 4)):
                project_k(g, ch, kb)
                evac_k_hi(g, ch, kb)
                evac_k_lo(g, ch, kb)

        split_ctx(0)
        K.chained = True
        m = layernorm(XNX, *m_end)
        K.chained = False
        prologue_k(0)
        stack_k(0)
        K.chained = True
        m_xt = transpose_to(XT, XNX, m)
        K.chained = False
        split_ctx(1)
        K.chained = True
        for c4 in range(NC):
            for c in range(NC):
                m = op("pe", lambda e, c=c, c4=c4: e.matmul(
                    bank(2 + c4, 0, 256), wq[:, c, 128 * c4:128 * c4 + 128], XT[:, c, :],
                    start=(c == 0), stop=(c == NC - 1)), *m_xt, m_wx, inc=(c == NC - 1))
            m = op("dve", lambda e, c4=c4: e.tensor_scalar(
                qf[:, 256 * c4:256 * c4 + 256], bank(2 + c4, 0, 256), BC[:, C_L1XQ + c4:C_L1XQ + c4 + 1], SCALE,
                ALU.add, ALU.mult), m)
            m_kbank[2 + c4] = m
        hl = [QHL[:, h].rearrange("p c j -> p (c j)") for h in range(2)]
        op("dve", lambda e: e.tensor_copy(hl[0], qf))
        m = op("dve", lambda e: e.tensor_tensor(hl[1], qf, hl[0].bitcast(F32), ALU.subtract))

        m_q = stack(QS, QHL[:, :], (0, 0, 1, 1), "d_q", m)
        m_pro = last("dve")

        K.chained = False
        prologue_k(1)
        stack_k(1)
        for n in range(2):
            for part in range(3):
                project_v(n, part)
            evac_v(n)
        for i in range(2):
            m_xb = op("dve", lambda e: e.tensor_tensor(X[:, i, :], X[:, i, :], BI[:, BSLOT[R_XO], :], ALU.add),
                      m_bi[R_XO])
        split_ctx(2)
        lo_due = None
        for k in range(NCH):
            t, c = k // 4, k % 4
            g = t // 2
            due_k = (g + 2, (k % 8) // 2) if k % 2 == 0 and g + 2 < NG else None
            n, part = (k + 12) // 6, (k + 12) % 6 // 2
            due_v = k % 2 and v_tile(n) < NT
            scores(k, 0)
            softmax(k, 0)
            if lo_due:
                evac_k_lo(*lo_due)
            if due_k:
                project_k(*due_k)
            elif due_v:
                project_v(n, part)
            scores(k, 1)
            if due_k:
                evac_k_hi(*due_k)
            softmax(k, 1)
            if due_v and part == 2:
                evac_v(n)
            if k >= 1:
                scale_v(k - 1)
            lo_due = due_k
            if k % 8 == 7 and g + 2 < NG:
                stack_k(g + 2)
            if c == 0 and (t + 2) % 6 in (4, 5) and t + 2 < NT:
                fetch_v(t + 2)
            if k % 8 == 5 and g + 3 < NG:
                split_ctx(g + 3)
            if k % 2 and k >= 3:
                mix(k - 3)
                mix(k - 2)
        scale_v(NCH - 1)
        mix(NCH - 2)
        mix(NCH - 1)
        K.chained = True
        m = m_pv[NCH - 1]
        for b in range(2):
            m2 = op("act" if b else "dve", lambda e, b=b: (
                e.activation(OT[:, 2 * b:2 * b + 2, :].rearrange("p c i -> p (c i)"), bank(6 + b), ACT.Copy) if b
                else e.tensor_copy(OT[:, 0:2, :].rearrange("p c i -> p (c i)"), bank(6))), m)
        m1 = last("dve")
        for i in range(2):
            for c in range(NC):
                m = op("pe", lambda e, i=i, c=c: e.matmul(
                    bank(2 + i), OT[:, c, 128 * i:128 * i + 128], wo[:, c, :],
                    start=(c == 0), stop=(c == NC - 1)), m1, m2, m_wo, m_ex[NCH - 1, 1], inc=(c == NC - 1))
            op("dve", lambda e, i=i: e.tensor_tensor(X[:, i, :], X[:, i, :], bank(2 + i), ALU.add), m)

        life.close()
        kv_life.close()
        life = ExitStack()
        RW = sb("RW", [P, 3, 4096], over=ctx)
        WL = RW[:, 1:3, :].rearrange("p r f -> p (r f)")
        AL = sb("AL", [P, 12288], over=life)
        QL = sb("QL", [P, 2048], over=life)
        m_wl1 = dma(lambda e: e.dma_start(WL, a["l1a"]), "d_wa", m_vp[NT - 1])
        m_wf, m_done, m_sp = {}, {}, {}
        NPC = 32

        def load_piece(n, *w):
            m_wf[n] = dma(lambda e: e.dma_start(RW[:, n % 3, :], a["l1f"][n]), f"d_f{n % 3}",
                          m_sp.get((n - 3, 1)), *w)

        load_piece(0)
        self_attention(WL, AL, QL[:, :], C_L1AQ, C_L1AK, R_AV, R_AO, m_wl1, mask1, [(0, 0), (1, 1)], 64)
        for n in (1, 2):
            load_piece(n, last("pe"))

        m_end = [last("pe"), last("dve"), last("act")]
        life.close()
        life = ctx
        WS1 = sb("WS1", [P, 2, 2, 2, 2048], F32R, life)
        XS1 = sb("XS1", [P, 2, NC, 256], F32R, life)
        HS1 = sb("HS1", [P, 4, 2, 256], F32R, life)
        HF1 = sb("HF1", [P, 4, 256], over=life)
        LN = sb("LN", [P, 2, D], over=life)
        MS = sb("MS", [P, 1024], over=life)
        ACC = sb("ACC", [P, 2, D], over=life)
        XNM = sb("XNM", [P, 2, D], over=life)
        lng, lnb = LN[:, 0], LN[:, 1]
        b2 = MS[0:8, 0:512]
        b1 = MS[:, 512:640]
        gw = MS[:, 640:672].rearrange("p (c n) -> p c n", c=NC)
        gbb = MS[:, 672:680]
        pT = MS[0:8, 768:1024].rearrange("p (i n) -> p i n", i=2)
        m_ln = dma(lambda e: e.dma_start(LN[:, :, :], a["lngb"].unsqueeze(0).to_broadcast([P, 2, D])), "d_w0", *m_end)
        m_b2 = dma(lambda e: e.dma_start(b2, a["b2"]), "d_x", *m_end)
        m_b1 = dma(lambda e: e.dma_start(MS[:, 512:680], a["l1g"]), "d_g", *m_end)
        m = layernorm(XNM, *m_end)
        m_xt = transpose_to(XT, XNM, m)
        m_xs = split_xt(XS1)
        m_start = [last("dve"), last("act"), last("pe")]
        K.chained = False
        m_g, m_h, m_dn, m_up, m_acc = {}, {}, {}, {}, {}

        def split1(n, w):
            src = RW[:, n % 3, 2048 * w:2048 * w + 2048]
            for p in range(2):
                z = slice(1024 * p, 1024 * p + 1024)
                hi = op("act", lambda e, z=z: e.activation(WS1[:, n % 2, w, 0, z], src[:, z], ACT.Copy), m_wf[n],
                        (m_dn if w else m_up).get(4 * (n - 2) + 3), *m_start)
                m_sp[n, w] = op("dve", lambda e, z=z: e.tensor_tensor(
                    WS1[:, n % 2, w, 1, z], src[:, z], WS1[:, n % 2, w, 0, z].bitcast(F32), ALU.subtract), hi)
            if w and n + 3 < NPC:
                load_piece(n + 3)

        def up1(n):
            pc, f = n // 4, n % 4
            q = 0
            for wh, xh in ((0, 0), (0, 1), (1, 0)):
                w1 = WS1[:, pc % 2, 0, wh, :].rearrange("p (c n) -> p c n", c=NC)
                for c in range(NC):
                    q += 1
                    m = op("pe", lambda e, c=c, w1=w1, xh=xh, q=q: e.matmul(
                        bank(n % 4, 0, 256), w1[:, c, 128 * f:128 * f + 128], XS1[:, xh, c, :],
                        start=(q == 1), stop=(q == 12)), m_sp[pc, 0], m_g.get(n - 4), m_xs, *m_start, inc=(q == 12))
            m_up[n] = m
            m_g[n] = op("act", lambda e: e.activation(
                HF1[:, n % 4, :], bank(n % 4, 0, 256), ACT.Gelu, bias=b1[:, n:n + 1]), m, m_b1, m_h.get(n - 4), *m_start)
            hi = op("dve", lambda e: e.tensor_copy(HS1[:, n % 4, 0, :], HF1[:, n % 4, :]), m_g[n], m_dn.get(n - 4))
            m_h[n] = op("pool", lambda e: e.tensor_tensor(
                HS1[:, n % 4, 1, :], HF1[:, n % 4, :], HS1[:, n % 4, 0, :].bitcast(F32), ALU.subtract), hi)

        def down1(n):
            pc, f = n // 4, n % 4
            x, fc = n // 16, n % 16
            for i in range(2):
                b = 4 + 2 * (x % 2) + i
                for q, (hh, wh) in enumerate(((0, 0), (0, 1), (1, 0))):
                    w2 = WS1[:, pc % 2, 1, wh, :].rearrange("p (f n) -> p f n", f=4)
                    m = op("pe", lambda e, i=i, b=b, q=q, hh=hh, w2=w2: e.matmul(
                        bank(b), HS1[:, n % 4, hh, 128 * i:128 * i + 128], w2[:, f, :],
                        start=(fc == 0 and q == 0), stop=(fc == 15 and q == 2)),
                        m_h[n], m_sp[pc, 1], m_acc.get((x - 2, i)), m_cb if x else None, inc=(i == 1 and q == 2))
            m_dn[n] = m
            if fc == 15:
                for i in range(2):
                    b = 4 + 2 * (x % 2) + i
                    m_acc[x, i] = op("dve", lambda e, i=i, b=b: e.scalar_tensor_tensor(
                        out=ACC[:, i, :], in0=bank(b), scalar=comb[:, i, x:x + 1], in1=ACC[:, i, :],
                        op0=ALU.mult, op1=ALU.add), m, m_acc.get((x - 1, i)), m_cb)

        split1(0, 0)
        split1(0, 1)
        up1(0)
        up1(1)
        K.chained = True
        for i in range(2):
            for c in range(NC):
                m = op("pe", lambda e, i=i, c=c: e.matmul(bank(7, 8 * i, 8), XT[:, c, 128 * i:128 * i + 128],
                                                          gw[:, c, :], start=(c == 0), stop=(c == NC - 1)),
                       *m_xt, m_b1, inc=(c == NC - 1))
        comb = small[:, 80:96].rearrange("p (i n) -> p i n", i=2)
        lg, rk, t8 = (small[:, o:o + 16] for o in (112, 128, 144))
        mxv, sv = small[:, 160:162], small[:, 162:164]
        l3, t3, b3 = (z.rearrange("p (i n) -> p i n", i=2) for z in (lg, t8, bank(7, 0, 16)))
        op("dve", lambda e: e.tensor_tensor(l3, b3, gbb.unsqueeze(1).to_broadcast([P, 2, 8]), ALU.add), m, last("act"))
        op("dve", lambda e: e.tensor_scalar(lg, lg, 1.0 / 0.9, None, ALU.mult))
        op("dve", lambda e: e.tensor_reduce(mxv, l3, axis=AX.X, op=ALU.max))
        m = op("dve", lambda e: e.tensor_tensor(t3, l3, mxv.unsqueeze(2).to_broadcast([P, 2, 8]), ALU.subtract))
        m = op("act", lambda e: e.activation(t8, t8, ACT.Exp), m)
        ranks(rk, lg, 8, 2, m_const)
        op("dve", lambda e: e.tensor_scalar(rk, rk, 2.0, None, ALU.is_lt))
        op("dve", lambda e: e.tensor_tensor(t8, t8, rk, ALU.mult), m)
        op("dve", lambda e: e.tensor_reduce(sv, t3, axis=AX.X, op=ALU.add))
        op("dve", lambda e: e.reciprocal(sv, sv))
        m_cb = op("dve", lambda e: e.tensor_tensor(comb, t3, sv.unsqueeze(2).to_broadcast([P, 2, 8]), ALU.mult))
        for i in range(2):
            m = op("pe", lambda e, i=i: e.transpose(PB[0:8, 6, 128 * i:128 * i + 128], comb[:, i, :], ident[:, :]), m_cb)
        m = op("dve", lambda e: e.tensor_copy(pT, PB[0:8, 6, 0:256].rearrange("p (i n) -> p i n", i=2)), m)
        for i in range(2):
            m2 = op("pe", lambda e, i=i: e.matmul(bank(6 + i), pT[:, i, :], b2, start=True, stop=True), m, m_b2)
            op("dve", lambda e, i=i: e.tensor_copy(ACC[:, i, :], bank(6 + i)), m2, *m_end)
        m_cb = last("dve")
        K.chained = False
        for n in range(128):
            if n > 1:
                up1(n)
            pc, f = n // 4, n % 4
            if pc + 1 < NPC and f in (1, 2):
                split1(pc + 1, f - 1)
            if n >= 2:
                down1(n - 2)
        down1(126)
        down1(127)
        K.chained = True
        for i in range(2):
            op("dve", lambda e, i=i: e.bn_stats(st[:, i, :], ACC[:, i, :]))
            m = op("dve", lambda e, i=i: e.bn_aggr(mv[:, i, :], st[:, i, :]))
        op("pool", lambda e: e.tensor_scalar(rstd[:, :], mv[:, :, 1], 1e-5, None, ALU.add), m)
        m = op("pool", lambda e: e.tensor_tensor(rstd[:, :], rstd[:, :], half[:, :], ALU.pow))
        for i in range(2):
            op("dve", lambda e, i=i: e.tensor_scalar(
                ACC[:, i, :], ACC[:, i, :], mv[:, i, 0:1], rstd[:, i:i + 1], ALU.subtract, ALU.mult), m)
            op("dve", lambda e, i=i: e.tensor_tensor(ACC[:, i, :], ACC[:, i, :], lng, ALU.mult), m_ln)
            op("dve", lambda e, i=i: e.tensor_tensor(ACC[:, i, :], ACC[:, i, :], lnb, ALU.add))
            m2 = op("dve", lambda e, i=i: e.tensor_tensor(X[:, i, :], X[:, i, :], ACC[:, i, :], ALU.add))
        m_out = dma(lambda e: e.dma_start(a["out"], X[:, :, :]), "d_out", m2)

        sems = {}
        for s in K.n:
            if s != "sp":
                sems[s] = ctx.enter_context(nc.semaphore("s_" + s))
        block = ctx.enter_context(nc.Block())

        @block.sync
        def _(e):
            K.play("sp", e, sems)
            e.wait_ge(sems["d_out"], m_out[1])

        @block.tensor
        def _(e):
            K.play("pe", e, sems)

        @block.scalar
        def _(e):
            K.play("act", e, sems)

        @block.vector
        def _(e):
            K.play("dve", e, sems)

        @block.gpsimd
        def _(e):
            K.play("pool", e, sems)


def layout(inp):
    f = {k: np.asarray(v) for k, v in inp.items()}

    def rows(w):
        return w.reshape(-1, P, w.shape[-1]).transpose(1, 0, 2)

    def cols(v):
        return v.reshape(-1, P).T

    def flat(*parts):
        return np.ascontiguousarray(np.concatenate([p.reshape(P, -1) for p in parts], axis=1))

    def rep(v):
        return np.broadcast_to(v.reshape(1, -1), (P, v.size))

    ctx = f["ctx_1024"].reshape(NG, GT, NC, P).transpose(0, 3, 2, 1).reshape(NG, P, NC * GT)
    w = f["L0_xattn_W"]
    qkv = f["L1_attn_w_qkv"].reshape(D, H, 3, 32).transpose(0, 2, 1, 3).reshape(D, 3 * D)
    bq = f["L1_attn_b_qkv"].reshape(H, 3, 32).transpose(1, 0, 2).reshape(3, D)
    b0 = f["L0_attn_bqkv"].reshape(3, D)
    w1 = np.concatenate([f["L0_ffn_w1"], f["L0_ffn_ws1"][None]])
    w2 = np.concatenate([f["L0_ffn_w2"], f["L0_ffn_ws2"][None]])
    w3 = np.concatenate([f["L0_ffn_w3"], f["L0_ffn_ws3"][None]])
    l0f = np.stack([flat(rows(w1[e].T), rows(w3[e].T), rows(w2[e].T)) for e in range(17)])
    l1f = []
    for e in range(8):
        for q in range(4):
            l1f.append(flat(rows(f["L1_ffn_w1"][e][:, 512 * q:512 * q + 512]),
                            rows(f["L1_ffn_w2"][e][512 * q:512 * q + 512])))
    return {
        "x": np.ascontiguousarray(f["x"].reshape(2, P, D).transpose(1, 0, 2)),
        "ctx": np.ascontiguousarray(ctx),
        "wkv": flat(rows(f["L1_xattn_Wk"]), rows(f["L1_xattn_Wv"])),
        "l0x": flat(rows(w[:, :D].T), rows(w[:, D:].T)),
        "l0a": flat(rows(f["L0_attn_Wqkv"].T), rows(f["L0_attn_Wo"].T)),
        "l1a": flat(rows(qkv), rows(f["L1_attn_w_o"])),
        "l1x": flat(rows(f["L1_xattn_Wq"]), rows(f["L1_xattn_Wo"])),
        "bcol": flat(cols(b0[0]), cols(b0[1]), cols(f["L1_xattn_bq"]), cols(f["L1_xattn_bk"]), cols(bq[0]), cols(bq[1])),
        "brow": np.stack([f["L0_xattn_b"], b0[2], f["L0_attn_bo"], f["L1_xattn_bv"], f["L1_xattn_bo"], bq[2],
                          f["L1_attn_b_o"]]),
        "l0g": flat(rows(f["L0_ffn_gate_w"].T), rep(f["L0_ffn_gate_bias"])),
        "l0f": l0f,
        "l1g": flat(cols(f["L1_ffn_b1"]), rows(f["L1_ffn_gate_w"]), rep(f["L1_ffn_gate_b"])),
        "l1f": np.stack(l1f),
        "b2": np.ascontiguousarray(f["L1_ffn_b2"]),
        "lngb": np.stack([f["L1_ffn_ln_g"], f["L1_ffn_ln_b"]]),
    }


def kernel(**inputs):
    import concourse.bacc as _bacc
    from concourse.bass_utils import run_bass_kernel_spmd as _run

    arrays = layout(inputs)
    nc = _bacc.Bacc("TRN2", target_bir_lowering=False, num_devices=1)
    aps = {k: nc.dram_tensor(f"in_{k}", v.shape, mybir.dt.from_np(v.dtype), kind="ExternalInput").ap()
           for k, v in arrays.items()}
    aps["out"] = nc.dram_tensor("out_x", (P, 2, D), F32, kind="ExternalOutput").ap()
    build(nc, aps)
    r = _run(nc, [{f"in_{k}": v for k, v in arrays.items()}], core_ids=[0])
    y = r.results[0]["out_x"]
    return np.ascontiguousarray(np.asarray(y).transpose(1, 0, 2)).reshape(1, 256, D)
```
